# Optimizing a Trainium2 kernel written in Bass

```python
import numpy as np
import jax
import jax.numpy as jnp

def _softmax(x, axis=-1):
    return jax.nn.softmax(x, axis=axis)

def _gelu(x):
    return jax.nn.gelu(x, approximate=True)

def _silu(x):
    return jax.nn.silu(x)

def _sigmoid(x):
    return jax.nn.sigmoid(x)

def _layernorm(x, axis=-1, eps=1e-05):
    m = jnp.mean(x, axis=axis, keepdims=True)
    v = jnp.var(x, axis=axis, keepdims=True)
    return (x - m) / jnp.sqrt(v + eps)

def _scatter_add(tgt, idx, src, axis=0):
    return tgt.at[idx].add(src)

def _segment_sum(src, seg, n):
    return jax.ops.segment_sum(src, seg, n)
kernel_name = 'mk_adj_preln_d4_adj_r2_dd4dc1'

def setup_inputs(seed: int=0):
    np.random.seed(seed)
    _w = jnp.asarray

    def _rec_inputs():
        import jax
        import jax.numpy as jnp
        _gk = jax.random.key(seed)
        x = 7.22e-05 + 1 * jax.random.normal(jax.random.fold_in(_gk, 1), (16, 512, 256), jnp.float32)
        _a = jax.random.bernoulli(jax.random.fold_in(_gk, 2), 0.015625, (16, 512, 512))
        _a = jnp.logical_or(_a, jnp.swapaxes(_a, -1, -2))
        _a = jnp.logical_or(_a, jnp.eye(512, dtype=bool))
        adj = _a.astype(jnp.int32)
        return (x, adj)
    x, adj = _rec_inputs()

    def _L0_gnn_setup():
        import jax, jax.numpy as jnp
        import numpy as np
        NEG_INF = -1000000000.0
        ALPHA = 0.1
        key = jax.random.key(seed)
        k1, k2, k3, k4, k5 = jax.random.split(key, 5)
        B, N, Din, Dout = (8, 1024, 256, 256)
        features = jax.random.normal(k1, (B, N, Din), dtype=jnp.float32)
        graph = jax.random.randint(k2, (B, N, N), 0, 2, dtype=jnp.int64)
        lim_w = 1.414 * np.sqrt(6.0 / (Din + Dout))
        w = jax.random.uniform(k3, (Din, Dout), jnp.float32, -lim_w, lim_w)
        lim_a = 1.414 * np.sqrt(6.0 / (Dout + 1))
        a1 = jax.random.uniform(k4, (Dout, 1), jnp.float32, -lim_a, lim_a)
        a2 = jax.random.uniform(k5, (Dout, 1), jnp.float32, -lim_a, lim_a)
        return {'features': features, 'graph': graph, 'w': w, 'a1': a1, 'a2': a2}
    _L0_gnn_all = _L0_gnn_setup()
    _L0_gnn_in = {k: v for k, v in _L0_gnn_all.items() if k in ('w', 'a1', 'a2')}
    del _L0_gnn_all

    def _L1_gnn_setup():
        import jax, jax.numpy as jnp
        import numpy as np
        B, N, D = (8, 512, 256)
        NH = 8
        DK = D // NH
        key = jax.random.key(seed)
        ks = jax.random.split(key, 6)
        x = jax.random.normal(ks[0], (B, N, D), dtype=jnp.float32)
        adj = jax.random.randint(ks[1], (B, N, N), 0, 2, dtype=jnp.int32)
        adj = jnp.maximum(adj, jnp.eye(N, dtype=jnp.int32)[None])
        s = 1.0 / np.sqrt(D)
        Wq = jax.random.normal(ks[2], (D, D), dtype=jnp.float32) * s
        Wk = jax.random.normal(ks[3], (D, D), dtype=jnp.float32) * s
        Wv = jax.random.normal(ks[4], (D, D), dtype=jnp.float32) * s
        Wo = jax.random.normal(ks[5], (D, D), dtype=jnp.float32) * s
        return {'x': x, 'adj': adj, 'Wq': Wq, 'Wk': Wk, 'Wv': Wv, 'Wo': Wo}
    _L1_gnn_all = _L1_gnn_setup()
    _L1_gnn_in = {k: v for k, v in _L1_gnn_all.items() if k in ('Wq', 'Wk', 'Wv', 'Wo')}
    del _L1_gnn_all

    def _L2_gnn_setup():
        import jax, jax.numpy as jnp
        import numpy as np
        B, N, IN_DIM, OUT_DIM, H = (512, 128, 256, 256, 8)
        D = OUT_DIM // H
        key = jax.random.key(seed)
        k1, k2, k3, k4 = jax.random.split(key, 4)
        x = jax.random.normal(k1, (B, N, IN_DIM), dtype=jnp.float32)
        adj = jax.random.randint(k2, (B, N, N), 0, 2, dtype=jnp.int32)
        W = jax.random.normal(k3, (IN_DIM, OUT_DIM), dtype=jnp.float32) / np.sqrt(IN_DIM).astype(np.float32)
        a = jax.random.normal(k4, (H, 2 * D), dtype=jnp.float32) * 0.1
        return {'x': x, 'adj': adj, 'W': W, 'a': a}
    _L2_gnn_all = _L2_gnn_setup()
    _L2_gnn_in = {k: v for k, v in _L2_gnn_all.items() if k in ('W', 'a')}
    del _L2_gnn_all

    def _L3_gnn_setup():
        import jax, jax.numpy as jnp
        import numpy as np
        B, N, H, NH = (8, 512, 256, 8)
        DK = H // NH
        key = jax.random.key(seed)
        ks = jax.random.split(key, 6)
        x = jax.random.normal(ks[0], (B, N, H), dtype=jnp.float32)
        adj = jax.random.randint(ks[1], (B, N, N), 0, 2, dtype=jnp.int32)
        adj = jnp.maximum(adj, jnp.eye(N, dtype=jnp.int32)[None])
        s = 1.0 / np.sqrt(H)
        Wq = jax.random.normal(ks[2], (H, H), dtype=jnp.float32) * s
        Wk = jax.random.normal(ks[3], (H, H), dtype=jnp.float32) * s
        Wv = jax.random.normal(ks[4], (H, H), dtype=jnp.float32) * s
        Wg = jax.random.normal(ks[5], (H, 2 * H), dtype=jnp.float32) * (1.0 / np.sqrt(2 * H))
        bg = jnp.zeros((H,), dtype=jnp.float32)
        return {'x': x, 'adj': adj, 'Wq': Wq, 'Wk': Wk, 'Wv': Wv, 'Wg': Wg, 'bg': bg}
    _L3_gnn_all = _L3_gnn_setup()
    _L3_gnn_in = {k: v for k, v in _L3_gnn_all.items() if k in ('Wq', 'Wk', 'Wv', 'Wg', 'bg')}
    del _L3_gnn_all
    return {'x': x, 'adj': adj, 'L0_gnn_w': _L0_gnn_in['w'], 'L0_gnn_a1': _L0_gnn_in['a1'], 'L0_gnn_a2': _L0_gnn_in['a2'], 'L1_gnn_Wq': _L1_gnn_in['Wq'], 'L1_gnn_Wk': _L1_gnn_in['Wk'], 'L1_gnn_Wv': _L1_gnn_in['Wv'], 'L1_gnn_Wo': _L1_gnn_in['Wo'], 'L2_gnn_W': _L2_gnn_in['W'], 'L2_gnn_a': _L2_gnn_in['a'], 'L3_gnn_Wq': _L3_gnn_in['Wq'], 'L3_gnn_Wk': _L3_gnn_in['Wk'], 'L3_gnn_Wv': _L3_gnn_in['Wv'], 'L3_gnn_Wg': _L3_gnn_in['Wg'], 'L3_gnn_bg': _L3_gnn_in['bg']}

def reference(x, adj, L0_gnn_w, L0_gnn_a1, L0_gnn_a2, L1_gnn_Wq, L1_gnn_Wk, L1_gnn_Wv, L1_gnn_Wo, L2_gnn_W, L2_gnn_a, L3_gnn_Wq, L3_gnn_Wk, L3_gnn_Wv, L3_gnn_Wg, L3_gnn_bg):
    import jax
    import jax.numpy as jnp

    def _L0_gnn_ref(features, graph, w, a1, a2):
        import jax, jax.numpy as jnp
        import numpy as np
        NEG_INF = -1000000000.0
        ALPHA = 0.1
        hidden = jnp.einsum('bni,io->bno', features, w)
        s1 = hidden @ a1
        s2 = hidden @ a2
        e = jax.nn.leaky_relu(s1 + jnp.swapaxes(s2, 1, 2), negative_slope=ALPHA)
        e = jnp.where(graph == 0, NEG_INF, e)
        attn = jax.nn.softmax(e, axis=-1)
        h_prime = jnp.einsum('bij,bjo->bio', attn, hidden)
        return jax.nn.elu(h_prime)

    def _L1_gnn_ref(x, adj, Wq, Wk, Wv, Wo):
        import jax, jax.numpy as jnp
        import numpy as np
        B, N, D = (8, 512, 256)
        NH = 8
        DK = D // NH
        b, n, d = x.shape
        sqrt_dk = jnp.asarray(np.sqrt(DK), dtype=x.dtype)

        def heads(t):
            return t.reshape(b, n, NH, DK).transpose(0, 2, 1, 3)
        q = heads(x @ Wq)
        k = heads(x @ Wk)
        v = heads(x @ Wv)
        scores = jnp.einsum('bhnd,bhmd->bhnm', q, k) / sqrt_dk
        mask = adj.astype(bool)[:, None]
        scores = jnp.where(mask, scores, -jnp.inf)
        attn = jax.nn.softmax(scores, axis=-1)
        out = jnp.einsum('bhnm,bhmd->bhnd', attn, v)
        out = out.transpose(0, 2, 1, 3).reshape(b, n, d)
        return jax.nn.relu(out) @ Wo

    def _L2_gnn_ref(x, adj, W, a):
        import jax, jax.numpy as jnp
        import numpy as np
        B, N, IN_DIM, OUT_DIM, H = (512, 128, 256, 256, 8)
        D = OUT_DIM // H
        b, n, _ = x.shape
        h = (x @ W).reshape(b, n, H, D)
        a1, a2 = (a[:, :D], a[:, D:])
        s_i = jnp.einsum('bnhd,hd->bnh', h, a1)
        s_j = jnp.einsum('bnhd,hd->bnh', h, a2)
        e = s_i[:, :, None, :] + s_j[:, None, :, :]
        e = jax.nn.leaky_relu(e, negative_slope=0.2)
        mask = (adj != 0)[..., None]
        e = jnp.where(mask, e, -jnp.inf)
        alpha = jax.nn.softmax(e, axis=2)
        alpha = jnp.nan_to_num(alpha, nan=0.0)
        out = jnp.einsum('bijh,bjhd->bihd', alpha, h).reshape(b, n, OUT_DIM)
        return jax.nn.elu(out)

    def _L3_gnn_ref(x, adj, Wq, Wk, Wv, Wg, bg):
        import jax, jax.numpy as jnp
        import numpy as np
        B, N, H, NH = (8, 512, 256, 8)
        DK = H // NH
        b, n, h = x.shape
        q = (x @ Wq.T).reshape(b, n, NH, DK)
        k = (x @ Wk.T).reshape(b, n, NH, DK)
        v = (x @ Wv.T).reshape(b, n, NH, DK)
        scores = jnp.einsum('bqhd,bkhd->bhqk', q, k) / jnp.sqrt(jnp.float32(DK))
        mask = (adj != 0)[:, None, :, :]
        scores = jnp.where(mask, scores, -jnp.inf)
        attn = jax.nn.softmax(scores, axis=-1)
        c = jnp.einsum('bhqk,bkhd->bqhd', attn, v).reshape(b, n, h)
        gate = jax.nn.sigmoid(jnp.concatenate([c, x], axis=2) @ Wg.T + bg)
        return gate * x + (1.0 - gate) * c
    h = jnp.maximum(_layernorm(x, axis=-1), 0.0)
    x = x + _L0_gnn_ref(h, adj, L0_gnn_w, L0_gnn_a1, L0_gnn_a2)
    h = jnp.maximum(_layernorm(x, axis=-1), 0.0)
    x = x + _L1_gnn_ref(h, adj, L1_gnn_Wq, L1_gnn_Wk, L1_gnn_Wv, L1_gnn_Wo)
    h = jnp.maximum(_layernorm(x, axis=-1), 0.0)
    x = x + _L2_gnn_ref(h, adj, L2_gnn_W, L2_gnn_a)
    h = jnp.maximum(_layernorm(x, axis=-1), 0.0)
    x = x + _L3_gnn_ref(h, adj, L3_gnn_Wq, L3_gnn_Wk, L3_gnn_Wv, L3_gnn_Wg, L3_gnn_bg)
    return x

_drawn_inputs = setup_inputs


def setup_inputs(seed=0):
    import zlib

    import numpy as np

    out = dict(_drawn_inputs(seed))
    spreads = {'L3_gnn_bg': (0.0, 0.611)}
    factors = {'L2_gnn_a': 2.71, 'L3_gnn_Wq': 3.8, 'L3_gnn_Wk': 3.584}
    for name, (base, spread) in spreads.items():
        noise = np.random.default_rng([zlib.crc32(name.encode()), seed]).standard_normal(out[name].shape)
        drawn = base * np.exp(spread * noise) if base else spread * noise
        out[name] = jnp.asarray(drawn.astype(out[name].dtype))
    for name, factor in factors.items():
        out[name] = (out[name] * factor).astype(out[name].dtype)
    return out
```

```python
from contextlib import ExitStack

import concourse.bass as bass
from concourse import mybir

F32 = mybir.dt.float32
F32R = mybir.dt.float32r
BF16 = mybir.dt.bfloat16
I32 = mybir.dt.int32
ALU = mybir.AluOpType
ACT = mybir.ActivationFunctionType
AX_X = mybir.AxisListType.X

P = 128
B, N, D = 16, 512, 256
H, DK = 8, 32
NT = N // P
DC = D // P
PAIRS = B // 2
EPS = 1e-5
MASKED = -1e30
BIG = 3.0e38
SCALE = float(DK) ** -0.5
SLOPE0, SLOPE2 = 0.1, 0.2
XW = DK + 1
VISITS = 8
LAG = 2


def layer(v):
    return (v % VISITS) // 2


def graph(v):
    return v % 2



def prepare(v):
    mask = [("mask", v)] if layer(v) == 0 else []
    norm = [("stats", v), ("norm", v), ("ht", v, 0), ("ht", v, 1)]
    if layer(v) == 0:
        return mask + norm + [("s2", v)] + [("v0", v, t) for t in range(NT)]
    if layer(v) == 2:
        return norm + [("rows", v), ("cols", v), ("vp", v, 0), ("vp", v, 1)]
    return norm + [("vp", v, 0), ("vp", v, 1), ("qk", v, 0, 0), ("qk", v, 0, 1)] \
        + ([("maskt", v, 0), ("maskt", v, 1)] if layer(v) == 1 else [])


def attend(v):
    if layer(v) == 0:
        out = [("emax", v)]
        for t in range(NT + 1):
            if t < NT:
                out.append(("e", v, t))
            if t >= 1:
                out += [("tr", v, t - 1), ("pv0", v, t - 1)]
        return out
    if layer(v) == 2:
        out = [("vx", v), ("mc", v)] + [("ms", v, t) for t in range(NT)]
        for h in range(H + 1):
            if h < H:
                out += [("bc", v, h)]
            if h >= 1:
                out += [("pc", v, h - 1)]
        return out
    out = []
    for n in range(4 * H + LAG):
        if n < 4 * H:
            out.append(("sc", v, n))
        if n >= LAG:
            out.append(("tr", v, n - LAG))
            if (n - LAG) % 8 == 7 and n - LAG < 31:
                out.append(("pv", v, (n - LAG) // 8))
                if (n - LAG) // 8 == 1:
                    out += [("rb", v, 0), ("no", v, 0)]
    return out


def finish(v):
    if layer(v) in (0, 2):
        return ([("z2", v)] if layer(v) == 2 else []) + [("elu", v)]
    last = [("pv", v, 3), ("rb", v, 1), ("no", v, 1)]
    if layer(v) == 1:
        return last + [("y", v, 0), ("y", v, 1)]
    return last + [("cn", v, 0), ("gate", v, 0), ("cn", v, 1), ("gate", v, 1)]


def merge(main, side, start, end):
    out, done = [], 0
    for n, step in enumerate(main):
        while done < len(side) and n >= start + (end - start) * done / len(side):
            out.append(side[done])
            done += 1
        out.append(step)
    return out + side[done:]


def turn():
    out = []
    for v in range(VISITS):
        main = attend(v)
        before = finish(v - 1) if v else []
        ahead = prepare((v + 1) % VISITS)
        if layer(v) in (1, 3):
            half = next(i for i, s in enumerate(main) if s == ("sc", v, 16))
            late = [("qk", v, 1, 0), ("qk", v, 1, 1)]
            first, second = main[:half], main[half:]
            k = next((i for i, s in enumerate(ahead) if s[0] in ("vp", "s2", "rows")), 0)
            out += merge(first, late + before + ahead[:k], 1, len(first))
            out += merge(second, ahead[k:], 3, len(second) - 1)
        else:
            out += merge(main, before + ahead, 1, len(main))
    return out + finish(VISITS - 1)


PROLOGUE = prepare(0)
TURN = turn()
TIMELINE = PROLOGUE + TURN

EVENTS = {
    "mask": ["mask_ready", "adj_used"], "maskt": ["maskt_sums", "maskt_ready"],
    "stats": ["stats_ready", "rstd_ready"], "norm": ["normed"],
    "ht": ["ht_made", "ht_ready"],
    "s2": ["s2_made", "s2_ready"], "v0": ["v_made", "v_ready"], "vp": ["v_made", "v_ready"],
    "qk": ["qk_made", "hi_ready", "lo_ready"],
    "rows": ["rows_made", "rows_ready"], "cols": ["cols_made", "cols_ready"],
    "vx": ["vx_ready"], "mc": ["mc_ready"], "ms": ["ms_made", "ms_ready"],
    "bc": ["bc_made", "edges_ready"], "pc": ["pc_made", "pc_ready", "head_ready"],
    "emax": ["shift_ready"], "e": ["scores_moved", "probs_ready"],
    "sc": ["scores_made", "scores_moved", "probs_ready"],
    "tr": ["probst_made"],
    "pv": ["out_made"], "pv0": ["out_made", "z_ready"],
    "rb": ["rinv_ready", "rb_made", "rb_ready"], "no": ["ot_ready"],
    "y": ["y_made", "x_ready"], "z2": ["z_ready"],
    "elu": ["elu_min", "elu_exp", "x_ready"],
    "cn": ["cn_made", "cn_used"], "gate": ["gate_made", "tanh_ready", "y_ready"],
}
def mover(step):
    return "act" if step[2] % 8 in (1, 4, 6) else "dve"


def events_of(step):
    own = EVENTS[step[0]]
    if step[0] == "tr":
        own = own + ["probst_by_" + mover(step)]
    return own


AT, PER, AHEAD = {}, {}, {}
for where, steps in (("prologue", PROLOGUE), ("turn", TURN)):
    for step in steps:
        for event in events_of(step):
            if where == "prologue":
                AHEAD[event] = AHEAD.get(event, 0) + 1
            else:
                AT[event, step] = PER.get(event, 0)
                PER[event] = PER.get(event, 0) + 1
CREDIT = dict(PER)

MISC = ("ht", "s2", "v0", "vp", "qk", "rows", "cols", "maskt", "ms", "rb", "y", "cn", "gate")
MISC_LAST = {"ht": "ht_ready", "s2": "s2_ready", "v0": "v_ready", "vp": "v_ready", "qk": "lo_ready",
             "rows": "rows_ready", "cols": "cols_ready", "maskt": "maskt_ready", "ms": "ms_ready",
             "rb": "rb_ready", "y": "x_ready", "cn": "cn_used", "gate": "tanh_ready"}
misc_turn = [s for s in TURN if s[0] in MISC]
misc_pro = [s for s in PROLOGUE if s[0] in MISC]
assert len(misc_turn) % 2 == 0


def build(nc, x_in, adj_in, w0, w0t, a12_in, wq1, wk1, wv1, wo1, w2, w2t, a_gat, wq3, wk3, wv3, wg3, bg, out):
    with ExitStack() as ctx:
        def sb(name, shape, dt=F32):
            return ctx.enter_context(nc.sbuf_tensor(name, shape, dt))

        def ps(name, shape, dt=F32):
            return ctx.enter_context(nc.psum_tensor(name, shape, dt))

        def sem(name):
            return ctx.enter_context(nc.semaphore(name))

        x = [sb(f"x{g}", [P, NT, D]) for g in range(2)]
        mask = [sb(f"mask{g}", [P, NT, N], BF16) for g in range(2)]
        edge_t = [sb(f"edge_t{g}", [P, NT, N], BF16) for g in range(2)]
        hn = [sb(f"hn{g}", [P, NT, D]) for g in range(2)]
        ht = [sb(f"ht{g}", [P, DC, N]) for g in range(2)]
        val = [sb(f"val{g}", [P, NT, D + 1]) for g in range(2)]
        s2b = [sb(f"s2b{g}", [P, N]) for g in range(2)]
        rows = s2b
        fa = [sb(f"fa{g}", [P, NT, H]) for g in range(2)]
        fb = [sb(f"fb{g}", [P, NT, H]) for g in range(2)]
        ea = [sb(f"ea{g}", [P, NT, H]) for g in range(2)]
        eb = [sb(f"eb{g}", [P, NT, H]) for g in range(2)]
        nsj = [sb(f"nsj{g}", [P, NT, H]) for g in range(2)]
        adj = [sb(f"adj{i}", [P, N], I32) for i in range(2)]
        bn = sb("bn", [P, NT, 6])
        mv = sb("mv", [P, NT, 2])
        rstd = sb("rstd", [P, NT])
        vare = sb("vare", [P, NT])
        power = sb("power", [P, NT])
        hi = [sb(f"hi{i}", [P, N], F32R) for i in range(2)]
        lo = [sb(f"lo{i}", [P, N], F32R) for i in range(2)]
        stack = [[sb(f"stack_{'qk'[w]}{b}", [96, 4, N], F32R) for w in range(2)] for b in range(2)]
        moved = [sb(f"moved{i}", [P, N]) for i in range(4)]
        probs = [sb(f"probs{i}", [P, N]) for i in range(4)]
        shift = sb("shift", [P, 4 * H])
        sums = [sb(f"sums{i}", [P, 2, 4, 4]) for i in range(2)]
        rinv = sb("rinv", [P, 4, 4])
        probs_t = [sb(f"probs_t{i}", [P, 4, NT, 2 * P]) for i in range(2)]
        edges = [probs_t[0][:, 2 * i:2 * i + 2, :, :].rearrange("p a b c -> p (a b c)")
                 .rearrange("p (t n) -> p t n", t=NT) for i in range(2)]
        rb = sb("rb", [P, N])
        ot = sb("ot", [P, DC, N])
        vx = sb("vx", [P, NT, H, 2 * XW])
        msum = sb("msum", [P, NT, H, XW])
        part = [sb(f"part{i}", [P, NT, 2 * XW]) for i in range(2)]
        diff = sb("diff", [P, NT, XW])
        numer = sb("numer", [P, NT, H, XW])
        z = sb("z", [P, NT, D])
        ez = sb("ez", [P, NT, D])
        tanh = ez[:, 0:2, :]
        small = sb("small", [P, 4 * NT])
        w_s = {n: sb("w_" + n, [P, DC, D]) for n in ("q1", "k1", "v1", "o1", "2", "q3", "k3", "v3")}
        w0_s = sb("w0_s", [P, DC, D + 1])
        w0_2 = sb("w0_2", [P, DC, P])
        wg_s = sb("wg_s", [P, 4, D])
        wt_s = ez
        a12 = sb("a12", [P, DC, 2])
        adiag = sb("adiag", [P, DC, 40])
        wa = sb("wa", [P, DC, 40])
        bg_s = sb("bg_s", [1, D])
        ident = sb("ident", [P, P])
        ident_b = sb("ident_b", [P, P], BF16)
        ones = sb("ones", [1, P])

        pscore = [ps(f"pscore{i}", [P, N]) for i in range(2)]
        ptrans = [ps(f"ptrans{i}", [P, N]) for i in range(2)]
        pout = [ps(f"pout{i}", [P, N]) for i in range(2)]
        pmisc = [ps(f"pmisc{i}", [P, N]) for i in range(2)]
        pmisc_b = [p[:, :].bitcast(BF16) for p in pmisc]

        S = {e: sem("s_" + e) for e in sorted({e for s in TIMELINE for e in events_of(s)})}
        x_loaded = [sem(f"x_loaded{g}") for g in range(2)]
        adj_loaded = [sem(f"adj_loaded{i}") for i in range(2)]
        out_stored = [sem(f"out_stored{g}") for g in range(2)]
        stacked = [[sem(f"stacked_{'qk'[w]}{b}") for w in range(2)] for b in range(2)]
        w_loaded = sem("w_loaded")
        credits = sem("credits")
        carried = sem("carried")
        setup_pool = sem("setup_pool")
        setup_pe = sem("setup_pe")
        setup_dve = sem("setup_dve")
        link_dve = sem("link_dve")
        link_act = sem("link_act")
        link_pool = sem("link_pool")

        class Walk:

            def __init__(self, eng, link=None):
                self.eng, self.link, self.linked, self.i, self.base = eng, link, 0, None, 0

            def at(self, event, step):
                here = TIMELINE_AT[self.place]
                n = AT[event, step] + 1
                if self.i is None:
                    return CREDIT[event] + n - PER[event] + AHEAD[event]
                if TURN_AT[step] > self.place - len(PROLOGUE):
                    n -= PER[event]
                return self.i * PER[event] + CREDIT[event] + AHEAD.get(event, 0) + n

            def wait(self, event, step, apart=False):
                value = self.at(event, step)
                (self.wait_apart if apart and self.i is not None else self.eng.wait_ge)(S[event], value)

            def wait_apart(self, semaphore, value):
                self.eng.wait_ge(semaphore, value)
                self.eng.sem_inc(carried, 1)

            def chain(self, instruction, apart=False):
                self.linked += 1
                instruction.then_inc(self.link, 1)
                turns = 0 if self.i is None else self.i * self.per
                (self.wait_apart if apart and self.i is not None else self.eng.wait_ge)(
                    self.link, turns + self.base + self.linked)

            def run(self, eng_loop, do, per=0):
                self.per = per
                for self.place, step in enumerate(PROLOGUE):
                    do(step)
                self.base, self.linked = self.linked, 0
                with eng_loop(0, PAIRS) as i:
                    self.i = i
                    for n, step in enumerate(TURN):
                        self.place = len(PROLOGUE) + n
                        do(step)
                assert self.linked == per, self.linked

        TURN_AT = {s: n for n, s in enumerate(TURN)}
        TIMELINE_AT = TIMELINE

        def misc_bank(w, step):
            seq = misc_pro if w.i is None else misc_turn
            n = seq.index(step)
            return n, n % 2

        def misc_free(w, step):
            n, bank = misc_bank(w, step)
            if w.i is None:
                if n >= 2:
                    w.wait(MISC_LAST[misc_pro[n - 2][0]], misc_pro[n - 2])
            else:
                last = misc_turn[n - 2]
                w.wait(MISC_LAST[last[0]], last)
                if n < 2:
                    w.wait(MISC_LAST[misc_pro[-1][0]], misc_pro[-1])
            return bank

        trs = [s for s in TURN if s[0] == "tr"]
        tr_at = {s: n for n, s in enumerate(trs)}
        scs = [s for s in TURN if s[0] in ("sc", "e")]
        sc_at = {s: n for n, s in enumerate(scs)}
        assert len(trs) % 4 == 0 and len(scs) % 4 == 0 and [s[1:] for s in trs] == [s[1:] for s in scs]
        moves = {s: "probst_by_" + mover(s) for s in trs}
        score_of = {s: ("sc" if layer(s[1]) in (1, 3) else "e",) + s[1:] for s in trs}

        def unpack(n):
            return n // 16, (n // 4) % 4, n % 4

        qks = [s for s in TURN if s[0] == "qk"]
        assert len(qks) % 2 == 0

        def adj_count(w, v, t):
            if w.i is None:
                return CREDIT_ADJ + t + 1
            return w.i * 2 * NT + CREDIT_ADJ + NT + (0 if graph(v) == 1 else NT) + t + 1

        CREDIT_ADJ = 2 * NT

        def last_scores(w, step):
            _, v, b, _ = step
            here = TURN_AT[step]
            mine = [s for s in scs if s[0] == "sc" and unpack(s[2])[0] == b]
            before = [s for s in mine if TURN_AT[s] < here]
            return before[-1] if before else mine[-1]

        def last_of(w, kind, step):
            mine = [s for s in TURN if s[0] == kind]
            before = [s for s in mine if TURN_AT[s] < TURN_AT[step]]
            return before[-1] if before else mine[-1]

        def stage_free(w, eng, step):
            n = qks.index(step)
            last = qks[n - 2]
            _, _, b, which = last
            done = [s for s in qks if s[2:] == (b, which)]
            count = 16 * 12 * (done.index(last) + 1)
            if w.i is None:
                return
            turns = w.i * (16 * 12 * len(done)) + 16
            if n - 2 < 0:
                return eng.wait_ge(stacked[b][which], turns)
            eng.wait_ge(stacked[b][which], turns + count)

        def move_probs_t(w, step, copy):
            _, v, n = step
            bank = tr_at[step] % 2
            w.wait("probst_made", step)
            if layer(v) == 0:
                if v == 0 and n < 2:
                    w.wait("out_made", ("pv", 7, 3))
                elif n >= 2:
                    w.wait("out_made", ("pv0", v, n - 2))
                else:
                    w.wait("out_made", ("pv0", 0, n + 2))
                dst = probs_t[1][:, n % 2, :, 0:P]
                src = ptrans[bank][:, :].rearrange("p (c q) -> p c q", c=NT)
                return copy(dst, src)
            b, t, head = unpack(n)
            buf = (n // 8) % 2
            if n % 8 < 2:
                if n // 8 >= 2:
                    w.wait("out_made", ("pv", v, n // 8 - 2))
                elif v % 2 == 1:
                    w.wait("out_made", ("pv", v - 1, n // 8 + 2))
                elif v == 2:
                    w.wait("out_made", ("pv0", 1, 3))
                else:
                    w.wait("pc_made", ("pc", v - 1, H - 1))
                    w.wait("out_made", ("pv", 3, 3))
            dst = probs_t[buf][:, head, :, (t % 2) * P:(t % 2 + 1) * P]
            return copy(dst, ptrans[bank][:, :].rearrange("p (c q) -> p c q", c=NT))

        block = ctx.enter_context(nc.Block())

        @block.sync
        def _(sp):
            for name, src in (("q1", wq1), ("k1", wk1), ("v1", wv1), ("o1", wo1), ("2", w2),
                              ("q3", wq3), ("k3", wk3), ("v3", wv3)):
                sp.dma_start(w_s[name][:, :, :], src.rearrange("(c p) n -> p c n", p=P)).then_inc(w_loaded, 16)
            sp.dma_start(w0_s[:, :, 0:D], w0.rearrange("(c p) n -> p c n", p=P)).then_inc(w_loaded, 16)
            sp.dma_start(wg_s[:, :, :], wg3.rearrange("(c p) n -> p c n", p=P)).then_inc(w_loaded, 16)
            sp.dma_start(wt_s[:, 0:2, :], w0t.rearrange("(c p) n -> p c n", p=P)).then_inc(w_loaded, 16)
            sp.dma_start(wt_s[:, 2:4, :], w2t.rearrange("(c p) n -> p c n", p=P)).then_inc(w_loaded, 16)
            sp.dma_start(a12[:, :, :], a12_in.rearrange("(c p) o -> p c o", p=P)).then_inc(w_loaded, 16)
            sp.dma_start(bg_s[:, :], bg.rearrange("(a n) -> a n", a=1)).then_inc(w_loaded, 16)
            sp.wait_ge(setup_pool, 1)
            for h in range(H):
                rows_h = slice(32 * (h % 4), 32 * (h % 4) + 32)
                sp.dma_start(adiag[rows_h, h // 4, h:h + 1],
                             a_gat[h, DK:2 * DK].rearrange("(p o) -> p o", o=1)).then_inc(w_loaded, 16)
                sp.dma_start(adiag[rows_h, h // 4, 32 + h:33 + h],
                             a_gat[h, 0:DK].rearrange("(p o) -> p o", o=1)).then_inc(w_loaded, 16)

            def load_x(index, g):
                sp.dma_start(x[g][:, :, :], x_in[index, :, :].rearrange("(t p) d -> p t d", p=P))\
                    .then_inc(x_loaded[g], 16)

            def do(step):
                kind, v = step[0], step[1]
                g = graph(v)
                if kind == "mask":
                    first = w.i is None
                    index = 0 if first else ((2 * w.i + 2) % B if g == 0 else 2 * w.i + 1)
                    for t in range(NT):
                        sp.wait_ge(S["adj_used"], adj_count(w, v, t - 2))
                        sp.dma_start(adj[t % 2][:, :], adj_in[index, t * P:(t + 1) * P, :])\
                            .then_inc(adj_loaded[t % 2], 16)
                if kind == "qk":
                    _, _, b, which = step
                    w.wait("hi_ready", step, apart=True)
                    w.wait("lo_ready", step, apart=True)
                    if not (w.i is None):
                        w.wait("scores_made", last_scores(w, step))
                    n = qks.index(step) % 2
                    parts = (hi, hi, lo) if which == 0 else (hi, lo, hi)
                    for r, src in enumerate(parts):
                        for head in range(4):
                            sp.dma_start(stack[b][which][32 * r:32 * r + 32, head, :].bitcast(F32),
                                         src[n][32 * head:32 * head + 32, :].bitcast(F32)).then_inc(stacked[b][which], 16)
                if kind == "gate" and step[2] == 1:
                    w.wait("y_ready", step)
                    where = 2 * w.i + g
                    sp.dma_start(out[where, :, :].rearrange("(t p) d -> p t d", p=P), hn[g][:, :, :])\
                        .then_inc(out_stored[g], 16)
                    load_x((2 * w.i + 2 + g) % B, g)

            load_x(0, 0)
            load_x(1, 1)
            sp.wait_ge(credits, 1)
            w = Walk(sp)
            w.run(sp.Fori, do)
            for g in range(2):
                sp.wait_ge(out_stored[g], 16 * (PAIRS + 1))
                sp.wait_ge(x_loaded[g], 16 * (PAIRS + 1))

        @block.gpsimd
        def _(pool):
            gp = nc.gpsimd
            for e in S:
                start = CREDIT_ADJ if e == "adj_used" else CREDIT[e]
                pool.sem_inc(S[e], start)
            for s in stacked[0] + stacked[1] + out_stored:
                pool.sem_inc(s, 16)
            pool.sem_inc(credits, 1)
            gp.memset(adiag[:, :, :], 0.0).then_inc(setup_pool, 1)
            gp.memset(ident[:, :], 0.0)
            gp.memset(ident_b[:, :], 0.0)
            gp.memset(power[:, :], -0.5)
            gp.memset(ones[:, :], 1.0).then_inc(setup_pool, 1)
            pool.wait_ge(setup_pool, 2)
            gp.affine_select(out=ident[:, :], in_=ident[:, :], compare_op=ALU.not_equal, fill=1.0,
                             base=0, pattern=[[-1, P]], channel_multiplier=1).then_inc(setup_pool, 1)
            gp.affine_select(out=ident_b[:, :], in_=ident_b[:, :], compare_op=ALU.not_equal, fill=1.0,
                             base=0, pattern=[[-1, P]], channel_multiplier=1).then_inc(setup_pool, 1)

            w = Walk(pool, link_pool)

            def do(step):
                kind, v = step[0], step[1]
                g = graph(v)
                if kind == "stats":
                    w.wait("stats_ready", step, apart=True)
                    w.chain(gp.tensor_scalar(vare[:, :], mv[:, :, 1], EPS, None, op0=ALU.add))
                    gp.tensor_tensor(rstd[:, :], vare[:, :], power[:, :], ALU.pow)\
                        .then_inc(S["rstd_ready"], 1)
                if kind == "pc":
                    h = step[2]
                    w.wait("pc_ready", step)
                    w.wait("head_ready", last_of(w, "pc", step))
                    w.wait("ms_ready", ("ms", v, NT - 1))
                    src = part[h % 2]
                    def col(t):
                        return t[g][:, :, h:h + 1].broadcast_to([P, NT, XW])
                    w.chain(gp.tensor_tensor(diff[:, :, :], msum[:, :, h, :], src[:, :, XW:2 * XW], ALU.subtract))
                    w.chain(gp.tensor_tensor(diff[:, :, :], diff[:, :, :], col(eb), ALU.mult))
                    w.chain(gp.tensor_tensor(numer[:, :, h, :], src[:, :, 0:XW], col(ea), ALU.mult))
                    gp.tensor_tensor(numer[:, :, h, :], numer[:, :, h, :], diff[:, :, :], ALU.add)\
                        .then_inc(S["head_ready"], 1)

            w.run(pool.Fori, do, per=sum({"stats": 1, "pc": 3}.get(s[0], 0) for s in TURN))

        @block.scalar
        def _(act):
            sc = nc.scalar
            w = Walk(act, link_act)
            act.wait_ge(credits, 1)

            def do(step):
                kind, v = step[0], step[1]
                g = graph(v)
                bank = misc_bank(w, step)[1] if kind in MISC else None
                if kind == "ht":
                    w.wait("ht_made", step)
                    sc.activation(ht[g][:, step[2], :], pmisc[bank][:, :], ACT.Relu).then_inc(S["ht_ready"], 1)
                if kind == "s2":
                    w.wait("s2_made", step)
                    sc.activation(s2b[g][:, :], pmisc[bank][:, :], ACT.Copy).then_inc(S["s2_ready"], 1)
                if kind == "v0":
                    w.wait("v_made", step)
                    sc.activation(val[g][:, step[2], :], pmisc[bank][:, 0:D + 1], ACT.Copy)\
                        .then_inc(S["v_ready"], 1)
                if kind == "vp":
                    j = step[2]
                    w.wait("v_made", step)
                    sc.activation(val[g][:, 2 * j:2 * j + 2, 0:D],
                                  pmisc[bank][:, :].rearrange("p (t d) -> p t d", t=2), ACT.Copy)\
                        .then_inc(S["v_ready"], 1)
                if kind == "qk":
                    w.wait("qk_made", step)
                    n = qks.index(step) % 2
                    stage_free(w, act, step)
                    sc.activation(hi[n][:, :], pmisc[bank][:, :], ACT.Copy).then_inc(S["hi_ready"], 1)
                if kind == "ms":
                    t = step[2]
                    w.wait("ms_made", step)
                    sc.activation(msum[:, t, :, :], pmisc[bank][:, 0:H * XW]
                                  .rearrange("p (h c) -> p h c", h=H), ACT.Copy).then_inc(S["ms_ready"], 1)
                if kind == "cols":
                    w.wait("cols_made", step)
                    pc = pmisc[bank][:, 0:NT * 40].rearrange("p (t c) -> p t c", t=NT)
                    w.chain(sc.activation(ea[g][:, :, :], pc[:, :, 32:40], ACT.Relu, scale=-1.0))
                    w.chain(sc.activation(eb[g][:, :, :], pc[:, :, 32:40], ACT.Relu))
                    sc.activation(fa[g][:, :, :], pc[:, :, 0:8], ACT.Exp)
                    sc.activation(fb[g][:, :, :], pc[:, :, 0:8], ACT.Exp, scale=SLOPE2)
                    sc.activation(nsj[g][:, :, :], pc[:, :, 0:8], ACT.Copy, scale=-1.0)
                    sc.activation(ea[g][:, :, :], ea[g][:, :, :], ACT.Exp, scale=SLOPE2 - 1.0)
                    sc.activation(eb[g][:, :, :], eb[g][:, :, :], ACT.Exp, scale=SLOPE2 - 1.0)\
                        .then_inc(S["cols_ready"], 1)
                if kind == "pc":
                    h = step[2]
                    w.wait("pc_made", step)
                    if h >= 2:
                        w.wait("head_ready", ("pc", v, h - 2))
                    sc.activation(part[h % 2][:, :, :], ptrans[h % 2][:, 0:NT * 2 * XW]
                                  .rearrange("p (t c) -> p t c", t=NT), ACT.Copy).then_inc(S["pc_ready"], 1)
                if kind == "e":
                    t = step[2]
                    n = sc_at[step]
                    w.wait("scores_moved", step)
                    if t == 0:
                        w.wait("shift_ready", ("emax", v))
                    w.wait("z_ready", ("pv0", 1 - v, t))
                    probs_free(w, n)
                    sc.activation(probs[n % 4][:, :], moved[n % 4][:, :], ACT.Exp,
                                  bias=small[:, 4 + t:5 + t], accum_out=small[:, 8 + t:9 + t])\
                        .then_inc(S["probs_ready"], 1)
                if kind == "sc":
                    n = sc_at[step]
                    b, t, head = unpack(step[2])
                    w.wait("scores_moved", step)
                    probs_free(w, n)
                    sc.activation(probs[n % 4][:, :], moved[n % 4][:, :], ACT.Exp, scale=-1.0,
                                  bias=shift[:, step[2]:step[2] + 1],
                                  accum_out=sums[g][:, b, t, head:head + 1]).then_inc(S["probs_ready"], 1)
                if kind == "tr" and mover(step) == "act":
                    move_probs_t(w, step, lambda o, i: sc.activation(o, i, ACT.Copy))\
                        .then_inc(S["probst_by_act"], 1)
                if kind == "rb":
                    w.wait("rb_made", step)
                    sc.activation(rb[:, :], pmisc[bank][:, :], ACT.Copy).then_inc(S["rb_ready"], 1)
                if kind == "elu":
                    w.wait("elu_min", step)
                    sc.activation(ez[:, :, :], ez[:, :, :], ACT.Exp).then_inc(S["elu_exp"], 1)
                if kind == "gate":
                    w.wait("gate_made", step)
                    w.wait("y_ready", last_of(w, "gate", step))
                    w.wait("x_ready", ("elu", 5))
                    sc.activation(tanh, pmisc[bank][:, :].rearrange("p (t d) -> p t d", t=2),
                                  ACT.Tanh, scale=0.5).then_inc(S["tanh_ready"], 1)

            def probs_free(w, n):
                w.wait("probst_made", trs[n - 4])

            w.run(act.Fori, do, per=sum({"cols": 2}.get(s[0], 0) for s in TURN))

        LINKS = {"stats": 1, "emax": 2, "e": 1, "rows": 2, "elu": 1, "gate": 1, "z2": 2, "pv0": 1, "rb": 1}

        @block.vector
        def _(dve):
            vec = nc.vector
            w = Walk(dve, link_dve)
            dve.wait_ge(credits, 1)
            dve.wait_ge(setup_pe, 1)
            vec.tensor_copy(w0_s[:, :, D], pmisc[0][:, 0:4].rearrange("p (c a) -> p c a", c=DC)[:, :, 0])\
                .then_inc(setup_dve, 1)
            for c in range(DC):
                vec.tensor_copy(w0_2[:, c, :], pmisc[0][:, 2 * c + 1:2 * c + 2].broadcast_to([P, P]))\
                    .then_inc(setup_dve, 1)
            vec.tensor_copy(wa[:, :, :], pmisc[0][:, 4:84].rearrange("p (c a) -> p c a", c=DC))\
                .then_inc(setup_dve, 1)

            def do(step):
                kind, v = step[0], step[1]
                g = graph(v)
                L = layer(v)
                bank = misc_bank(w, step)[1] if kind in MISC else None
                turns = 0 if w.i is None else w.i
                if kind == "mask":
                    for t in range(NT):
                        first = w.i is None
                        seen = (t // 2 + 1) if first else turns * 4 + 2 + (0 if g == 1 else 2) + t // 2 + 1
                        dve.wait_ge(adj_loaded[t % 2], 16 * seen)
                        ins = vec.tensor_scalar(mask[g][:, t, :], adj[t % 2][:, :], 0.0, MASKED,
                                                op0=ALU.is_equal, op1=ALU.mult)
                        ins.then_inc(S["adj_used"], 1)
                    w.eng.wait_ge(S["adj_used"], adj_count(w, v, NT - 1))
                    vec.memset(small[:, 15:16], 0.0).then_inc(S["mask_ready"], 1)
                if kind == "maskt":
                    j = step[2]
                    w.wait("maskt_sums", step)
                    vec.tensor_scalar(edge_t[g][:, 2 * j:2 * j + 2, :],
                                      pmisc_b[bank].rearrange("p (t n) -> p t n", t=2),
                                      0.0, None, op0=ALU.is_equal).then_inc(S["maskt_ready"], 1)
                if kind == "stats":
                    if L == 0:
                        dve.wait_ge(x_loaded[g], 16 if w.i is None else (w.i + (2 if g == 0 else 1)) * 16)
                    else:
                        w.wait("x_ready", ("y", v - 2, 1) if L == 2 else ("elu", v - 2))
                    w.wait("rstd_ready", last_of(w, "stats", step)) if w.i is not None else None
                    w.wait("normed", last_of(w, "norm", step)) if w.i is not None else None
                    for t in range(NT):
                        ins = vec.bn_stats(bn[:, t, :], x[g][:, t, :])
                    w.chain(ins, apart=True)
                    for t in range(NT):
                        ins = vec.bn_aggr(mv[:, t, :], bn[:, t, :])
                    ins.then_inc(S["stats_ready"], 1)
                if kind == "norm":
                    w.wait("rstd_ready", ("stats", v))
                    if L == 0:
                        if w.i is not None:
                            dve.wait_ge(out_stored[g], 16 * (w.i + (2 if g == 0 else 1)))
                    for t in range(NT):
                        ins = vec.tensor_scalar(hn[g][:, t, :], x[g][:, t, :], mv[:, t, 0:1], rstd[:, t:t + 1],
                                                op0=ALU.subtract, op1=ALU.mult)
                    ins.then_inc(S["normed"], 1)
                if kind == "qk":
                    n = qks.index(step) % 2
                    stage_free(w, dve, step)
                    w.wait("hi_ready", step)
                    vec.tensor_tensor(lo[n][:, :], pmisc[bank][:, :], hi[n][:, :].bitcast(F32), ALU.subtract)\
                        .then_inc(S["lo_ready"], 1)
                if kind == "rows":
                    w.wait("rows_made", step)
                    pr = pmisc[bank]
                    vec.tensor_reduce(small[0:8, 12:13], pr[0:8, :], axis=AX_X, op=ALU.max)
                    w.chain(vec.tensor_reduce(small[32:40, 12:13], pr[0:8, :], axis=AX_X, op=ALU.max))
                    w.chain(vec.tensor_scalar(rows[g][0:8, :], pr[0:8, :], small[0:8, 12:13], None,
                                              op0=ALU.subtract))
                    vec.tensor_scalar(rows[g][32:40, :], pr[32:40, :], small[32:40, 12:13], None,
                                      op0=ALU.add).then_inc(S["rows_ready"], 1)
                if kind == "emax":
                    w.wait("s2_ready", ("s2", v))
                    w.wait("v_ready", ("v0", v, NT - 1))
                    w.wait("mask_ready", ("mask", v))
                    for t in range(NT):
                        first = scs[(sc_at[("e", v, 0)] + t) - 4]
                        w.wait("probs_ready", first, apart=True)
                        ins = vec.tensor_tensor_reduce(out=moved[(sc_at[("e", v, 0)] + t) % 4][:, :],
                                                       in0=s2b[g][:, :], in1=mask[g][:, t, :], scale=1.0,
                                                       scalar=-BIG, op0=ALU.add, op1=ALU.max,
                                                       accum_out=small[:, t:t + 1])
                    w.chain(ins)
                    s1 = val[g][:, :, D]
                    w.chain(vec.scalar_tensor_tensor(out=small[:, 0:4], in0=small[:, 0:4], scalar=-1.0,
                                                     in1=s1, op0=ALU.mult, op1=ALU.subtract))
                    vec.scalar_tensor_tensor(out=small[:, 4:8], in0=small[:, 0:4], scalar=SLOPE0,
                                             in1=small[:, 0:4], op0=ALU.mult, op1=ALU.min)\
                        .then_inc(S["shift_ready"], 1)
                if kind == "e":
                    t = step[2]
                    buf = moved[sc_at[step] % 4]
                    w.chain(vec.tensor_scalar(buf[:, :], buf[:, :], val[g][:, t, D:D + 1], None, op0=ALU.add))
                    vec.scalar_tensor_tensor(out=buf[:, :], in0=buf[:, :], scalar=SLOPE0, in1=buf[:, :],
                                             op0=ALU.mult, op1=ALU.max).then_inc(S["scores_moved"], 1)
                if kind == "sc":
                    n = sc_at[step]
                    b, t, head = unpack(step[2])
                    if step[2] == 0:
                        w.wait("mask_ready", ("mask", g))
                    w.wait("probs_ready", scs[n - 4])
                    w.wait("scores_made", step, apart=True)
                    vec.tensor_tensor_reduce(out=moved[n % 4][:, :], in0=pscore[n % 2][:, :],
                                             in1=mask[g][:, t, :], scale=-SCALE, scalar=BIG,
                                             op0=ALU.add, op1=ALU.min,
                                             accum_out=shift[:, step[2]:step[2] + 1])\
                        .then_inc(S["scores_moved"], 1)
                if kind == "tr" and mover(step) == "dve":
                    move_probs_t(w, step, vec.tensor_copy).then_inc(S["probst_by_dve"], 1)
                if kind == "rb":
                    b = step[2]
                    w.wait("probs_ready", ("sc", v, 16 * b + 15))
                    w.chain(vec.reciprocal(rinv[:, :, :], sums[g][:, b, :, :]))
                    rep = rinv[:, :, :].rearrange("p t (h o) -> p (t h) o", o=1).broadcast_to([P, 16, DK])
                    vec.tensor_copy(rb[:, :].rearrange("p (a d) -> p a d", d=DK), rep)\
                        .then_inc(S["rinv_ready"], 1)
                if kind == "no":
                    b = step[2]
                    w.wait("out_made", ("pv", v, 2 * b + 1))
                    w.wait("rb_ready", ("rb", v, b))
                    last = v - 1 if v % 2 == 1 else {2: 7, 6: 3}[v]
                    w.wait(*(("gate_made", ("gate", last, 1)) if layer(last) == 3 else ("y_made", ("y", last, 1))))
                    if L == 1:
                        ins = vec.scalar_tensor_tensor(out=ot[:, b, :], in0=pout[b][:, :], scalar=0.0,
                                                       in1=rb[:, :], op0=ALU.max, op1=ALU.mult)
                    else:
                        ins = vec.tensor_tensor(ot[:, b, :], pout[b][:, :], rb[:, :], ALU.mult)
                    ins.then_inc(S["ot_ready"], 1)
                if kind == "y":
                    j = step[2]
                    w.wait("y_made", step)
                    half = x[g][:, 2 * j:2 * j + 2, :]
                    vec.tensor_tensor(half, pmisc[bank][:, :].rearrange("p (t d) -> p t d", t=2), half, ALU.add)\
                        .then_inc(S["x_ready"], 1)
                if kind == "pv0":
                    t = step[2]
                    w.wait("out_made", step)
                    w.wait("probs_ready", ("e", v, t))
                    w.chain(vec.reciprocal(small[:, 13:14], small[:, 8 + t:9 + t]))
                    vec.tensor_scalar(z[:, t, :], pout[t % 2][:, 0:D], small[:, 13:14], None, op0=ALU.mult)\
                        .then_inc(S["z_ready"], 1)
                if kind == "vx":
                    w.wait("v_ready", ("vp", v, 1))
                    w.wait("cols_ready", ("cols", v))
                    w.wait("pc_made", ("pc", {4: 5, 5: 4}[v], H - 1))
                    for t in range(NT):
                        src = val[g][:, t, 0:D].rearrange("p (h d) -> p h d", h=H)
                        for k, f in enumerate((fa, fb)):
                            c0 = k * XW
                            fac = f[g][:, t, :].rearrange("p (h o) -> p h o", o=1).broadcast_to([P, H, DK])
                            vec.tensor_tensor(vx[:, t, :, c0:c0 + DK], src, fac, ALU.mult)
                    for k, f in enumerate((fa, fb)):
                        ins = vec.tensor_copy(vx[:, :, :, k * XW + DK], f[g][:, :, :])
                    ins.then_inc(S["vx_ready"], 1)
                if kind == "mc":
                    w.wait("maskt_ready", ("maskt", 2 + g, 1))
                    w.wait("pc_made", ("pc", {4: 5, 5: 4}[v], H - 1))
                    w.wait("out_made", ("pv", 3, 2))
                    vec.tensor_copy(edges[0], edge_t[g][:, :, :]).then_inc(S["mc_ready"], 1)
                if kind == "bc":
                    h = step[2]
                    dst = edges[(h + 1) % 2]
                    w.wait("bc_made", step)
                    if h == 1:
                        w.wait("ms_made", ("ms", v, NT - 1))
                    if h >= 2:
                        w.wait("pc_made", ("pc", v, h - 2))
                    for t in range(NT):
                        ins = vec.scalar_tensor_tensor(out=dst[:, t, :], in0=pscore[h % 2][:, :],
                                                       scalar=nsj[g][:, t, h:h + 1], in1=edge_t[g][:, t, :],
                                                       op0=ALU.is_gt, op1=ALU.mult)
                    ins.then_inc(S["edges_ready"], 1)
                if kind == "z2":
                    w.wait("head_ready", ("pc", v, H - 1))
                    den = ez[:, 0, 0:NT * H].rearrange("p (t h) -> p t h", t=NT)
                    w.wait("elu_exp", last_of(w, "elu", ("elu", v)))
                    w.wait("x_ready", ("elu", v - 1) if v == 5 else ("elu", 1))
                    w.chain(vec.tensor_scalar(den, numer[:, :, :, DK], 1e-37, None, op0=ALU.max))
                    w.chain(vec.reciprocal(den, den))
                    for t in range(NT):
                        fac = den[:, t, :].rearrange("p (h o) -> p h o", o=1).broadcast_to([P, H, DK])
                        ins = vec.tensor_tensor(z[:, t, :].rearrange("p (h d) -> p h d", h=H),
                                                numer[:, t, :, 0:DK], fac, ALU.mult)
                    ins.then_inc(S["z_ready"], 1)
                if kind == "elu":
                    w.wait("z_ready", ("z2", v) if L == 2 else ("pv0", v, NT - 1))
                    w.wait("tanh_ready", ("gate", 7, 1))
                    vec.tensor_scalar(ez[:, :, :], z[:, :, :], 0.0, None, op0=ALU.min).then_inc(S["elu_min"], 1)
                    w.wait("elu_exp", step)
                    w.chain(vec.scalar_tensor_tensor(out=x[g][:, :, :], in0=ez[:, :, :], scalar=-1.0,
                                                     in1=x[g][:, :, :], op0=ALU.add, op1=ALU.add))
                    vec.scalar_tensor_tensor(out=x[g][:, :, :], in0=z[:, :, :], scalar=0.0,
                                             in1=x[g][:, :, :], op0=ALU.max, op1=ALU.add)\
                        .then_inc(S["x_ready"], 1)
                if kind == "cn":
                    j = step[2]
                    w.wait("cn_made", step)
                    c = pmisc[bank][:, :].rearrange("p (t d) -> p t d", t=2)
                    sl = slice(2 * j, 2 * j + 2)
                    vec.scalar_tensor_tensor(out=hn[g][:, sl, :], in0=hn[g][:, sl, :], scalar=0.0, in1=c,
                                             op0=ALU.max, op1=ALU.subtract)
                    vec.tensor_tensor(x[g][:, sl, :], c, x[g][:, sl, :], ALU.add).then_inc(S["cn_used"], 1)
                if kind == "gate":
                    j = step[2]
                    w.wait("tanh_ready", step)
                    w.wait("cn_used", ("cn", v, j))
                    sl = slice(2 * j, 2 * j + 2)
                    w.chain(vec.scalar_tensor_tensor(out=hn[g][:, sl, :], in0=tanh, scalar=1.0,
                                                     in1=hn[g][:, sl, :], op0=ALU.add, op1=ALU.mult))
                    vec.scalar_tensor_tensor(out=hn[g][:, sl, :], in0=hn[g][:, sl, :], scalar=0.5,
                                             in1=x[g][:, sl, :], op0=ALU.mult, op1=ALU.add)\
                        .then_inc(S["y_ready"], 1)

            w.run(dve.Fori, do, per=sum(LINKS.get(s[0], 0) for s in TURN))

        @block.tensor
        def _(pe):
            mm = nc.tensor.matmul
            w = Walk(pe)
            pe.wait_ge(w_loaded, 16 * (14 + 2 * H))
            pe.wait_ge(credits, 1)
            for c in range(DC):
                for o in range(DC):
                    mm(pmisc[0][:, 2 * c:2 * c + 2], wt_s[:, o, P * c:P * c + P], a12[:, o, :],
                       start=o == 0, stop=o == DC - 1)
            for c in range(DC):
                for o in range(DC):
                    last = mm(pmisc[0][:, 4 + 40 * c:44 + 40 * c], wt_s[:, 2 + o, P * c:P * c + P],
                              adiag[:, o, :], start=o == 0, stop=o == DC - 1)
            last.then_inc(setup_pe, 1)
            pe.wait_ge(setup_dve, 4)
            pe.wait_ge(setup_pool, 4)

            def do(step):
                kind, v = step[0], step[1]
                g = graph(v)
                L = layer(v)
                bank = misc_free(w, step) if kind in MISC else None
                if kind == "ht":
                    j = step[2]
                    w.wait("normed", ("norm", v))
                    for t in range(NT):
                        last = nc.tensor.transpose(pmisc[bank][:, P * t:P * t + P],
                                                   hn[g][:, t, P * j:P * j + P], ident[:, :])
                    last.then_inc(S["ht_made"], 1)
                if kind in ("s2", "v0", "vp", "rows", "qk"):
                    w.wait("ht_ready", ("ht", v, 1))
                if kind == "s2":
                    for c in range(DC):
                        last = mm(pmisc[bank][:, :], w0_2[:, c, :], ht[g][:, c, :], start=c == 0, stop=c == DC - 1)
                    last.then_inc(S["s2_made"], 1)
                if kind == "v0":
                    t = step[2]
                    for c in range(DC):
                        last = mm(pmisc[bank][:, 0:D + 1], ht[g][:, c, P * t:P * t + P], w0_s[:, c, :],
                                  start=c == 0, stop=c == DC - 1)
                    last.then_inc(S["v_made"], 1)
                if kind == "vp":
                    wv = w_s[{1: "v1", 2: "2", 3: "v3"}[L]]
                    for k in range(2):
                        t = 2 * step[2] + k
                        for c in range(DC):
                            last = mm(pmisc[bank][:, D * k:D * k + D], ht[g][:, c, P * t:P * t + P], wv[:, c, :],
                                      start=c == 0, stop=c == DC - 1)
                    last.then_inc(S["v_made"], 1)
                if kind == "qk":
                    _, _, b, which = step
                    wp = w_s["qk"[which] + str(L)]
                    for c in range(DC):
                        last = mm(pmisc[bank][:, :], wp[:, c, P * b:P * b + P], ht[g][:, c, :],
                                  start=c == 0, stop=c == DC - 1)
                    last.then_inc(S["qk_made"], 1)
                if kind == "rows":
                    for c in range(DC):
                        last = mm(pmisc[bank][0:40, :], wa[:, c, :], ht[g][:, c, :], start=c == 0, stop=c == DC - 1)
                    last.then_inc(S["rows_made"], 1)
                if kind == "cols":
                    w.wait("rows_ready", ("rows", v), apart=True)
                    for t in range(NT):
                        last = nc.tensor.transpose(pmisc[bank][:, 40 * t:40 * t + 40],
                                                   rows[g][0:40, P * t:P * t + P], ident[0:40, 0:40])
                    last.then_inc(S["cols_made"], 1)
                if kind == "maskt":
                    j = step[2]
                    w.wait("mask_ready", ("mask", g))
                    for k in range(2):
                        for t in range(NT):
                            key = 2 * j + k
                            last = nc.tensor.transpose(pmisc_b[bank][:, N * k + P * t:N * k + P * t + P],
                                                       mask[g][:, t, P * key:P * key + P], ident_b[:, :])
                    last.then_inc(S["maskt_sums"], 1)
                if kind == "sc":
                    n = sc_at[step]
                    b, t, head = unpack(step[2])
                    if step[2] % 16 == 0:
                        for which in range(2):
                            same = [s for s in qks if s[2:] == (b, which)]
                            seen = same.index(("qk", v, b, which)) + 1
                            pe.wait_ge(stacked[b][which], w.i * (16 * 12 * len(same)) + 16 * 12 * seen + 16)
                    if step[2] >= 2:
                        w.wait("scores_moved", ("sc", v, step[2] - 2))
                    elif v % 2 == 1:
                        w.wait("scores_moved", ("sc", v - 1, 30 + step[2]))
                    else:
                        w.wait("scores_moved", ("sc", {2: 7, 6: 3}[v], 30 + step[2]))
                        w.wait("edges_ready", ("bc", 5, 6 + step[2]))
                    mm(pscore[n % 2][:, :], stack[b][0][:, head, P * t:P * t + P], stack[b][1][:, head, :],
                       start=True, stop=True).then_inc(S["scores_made"], 1)
                if kind == "tr":
                    at = tr_at[step]
                    w.wait("probs_ready", score_of[step])
                    last_tr = trs[at - 2]
                    w.wait(moves[last_tr], last_tr)
                    w.wait("pc_ready", ("pc", 5, H - 2 + at % 2))
                    for c in range(NT):
                        last = nc.tensor.transpose(ptrans[at % 2][:, P * c:P * c + P],
                                                   probs[sc_at[score_of[step]] % 4][:, P * c:P * c + P],
                                                   ident[:, :])
                    last.then_inc(S["probst_made"], 1)
                if kind == "pv0":
                    t = step[2]
                    w.wait(moves["tr", v, t], ("tr", v, t))
                    w.wait("v_ready", ("v0", v, NT - 1))
                    w.wait("ot_ready", ("no", 7, t % 2))
                    if t >= 2:
                        w.wait("z_ready", ("pv0", v, t - 2))
                    elif v == 1:
                        w.wait("z_ready", ("pv0", 0, t + 2))
                    for c in range(NT):
                        last = mm(pout[t % 2][:, 0:D], probs_t[1][:, t % 2, c, 0:P], val[g][:, c, 0:D],
                                  start=c == 0, stop=c == NT - 1)
                    last.then_inc(S["out_made"], 1)
                if kind == "pv":
                    quarter = step[2]
                    b, half = quarter // 2, quarter % 2
                    mine = [s for s in trs if s[1] == v and s[2] // 8 == quarter]
                    for last in {moves[s]: s for s in mine}.values():
                        w.wait(moves[last], last)
                    w.wait("v_ready", ("vp", v, 1))
                    if half == 0:
                        if v % 2 == 1:
                            w.wait("ot_ready", ("no", v - 1, b))
                        else:
                            w.wait("ot_ready", ("no", {2: 7, 6: 3}[v], b))
                            w.wait("z_ready", ("pv0", 1, 2 + b))
                    for c in range(NT):
                        for head in range(4):
                            col = DK * (4 * b + head)
                            last = mm(pout[b][32 * head:32 * head + 32, 2 * P * half:2 * P * (half + 1)],
                                      val[g][:, c, col:col + DK], probs_t[quarter % 2][:, head, c, :],
                                      start=c == 0, stop=c == NT - 1, skip_group_check=True)
                    last.then_inc(S["out_made"], 1)
                if kind == "rb":
                    w.wait("rinv_ready", step)
                    for t in range(NT):
                        last = nc.tensor.transpose(pmisc[bank][:, P * t:P * t + P], rb[:, P * t:P * t + P],
                                                   ident[:, :])
                    last.then_inc(S["rb_made"], 1)
                if kind == "y":
                    w.wait("ot_ready", ("no", v, 1))
                    for k in range(2):
                        t = 2 * step[2] + k
                        for c in range(DC):
                            last = mm(pmisc[bank][:, D * k:D * k + D], ot[:, c, P * t:P * t + P],
                                      w_s["o1"][:, c, :], start=c == 0, stop=c == DC - 1)
                    last.then_inc(S["y_made"], 1)
                if kind == "cn":
                    w.wait("ot_ready", ("no", v, 1))
                    for k in range(2):
                        t = 2 * step[2] + k
                        for c in range(DC):
                            at = D * k + P * c
                            last = nc.tensor.transpose(pmisc[bank][:, at:at + P], ot[:, c, P * t:P * t + P],
                                                       ident[:, :])
                    last.then_inc(S["cn_made"], 1)
                if kind == "gate":
                    w.wait("ot_ready", ("no", v, 1))
                    for k in range(2):
                        t = 2 * step[2] + k
                        dst = pmisc[bank][:, D * k:D * k + D]
                        mm(dst, ones[0:1, :], bg_s[0:1, :], start=True, stop=False)
                        for c in range(4):
                            src = ot[:, c, P * t:P * t + P] if c < 2 else ht[g][:, c - 2, P * t:P * t + P]
                            last = mm(dst, src, wg_s[:, c, :], start=False, stop=c == 3)
                    last.then_inc(S["gate_made"], 1)
                if kind == "ms":
                    t = step[2]
                    w.wait("mc_ready", ("mc", v))
                    w.wait("vx_ready", ("vx", v))
                    for c in range(NT):
                        last = mm(pmisc[bank][:, 0:H * XW], edges[0][:, c, P * t:P * t + P],
                                  vx[:, c, :, XW:2 * XW], start=c == 0, stop=c == NT - 1)
                    last.then_inc(S["ms_made"], 1)
                if kind == "bc":
                    h = step[2]
                    w.wait("rows_ready", ("rows", v))
                    if h >= 2:
                        w.wait("edges_ready", ("bc", v, h - 2))
                    elif v == 5:
                        w.wait("edges_ready", ("bc", 4, 6 + h))
                    else:
                        w.wait("scores_moved", ("sc", 3, 30 + h))
                    mm(pscore[h % 2][:, :], ident[0:40, 32 + h:33 + h].broadcast_to([40, P]),
                       rows[g][0:40, :], start=True, stop=True)\
                        .then_inc(S["bc_made"], 1)
                if kind == "pc":
                    h = step[2]
                    w.wait("edges_ready", ("bc", v, h))
                    if h >= 2:
                        w.wait("pc_ready", ("pc", v, h - 2))
                    elif v == 5:
                        w.wait("pc_ready", ("pc", 4, 6 + h))
                    else:
                        w.wait(moves["tr", 3, 30 + h], ("tr", 3, 30 + h))
                    src = edges[(h + 1) % 2]
                    for t in range(NT):
                        for c in range(NT):
                            last = mm(ptrans[h % 2][:, 2 * XW * t:2 * XW * (t + 1)], src[:, c, P * t:P * t + P],
                                      vx[:, c, h, :], start=c == 0, stop=c == NT - 1)
                    last.then_inc(S["pc_made"], 1)

            w.run(pe.Fori, do)



def kernel(**inputs):
    import numpy as np
    import concourse.bacc as bacc
    from concourse.bass_utils import run_bass_kernel_spmd

    plain = lambda name: np.ascontiguousarray(inputs[name])
    turned = lambda name: np.ascontiguousarray(np.asarray(inputs[name]).T)
    arrays = {
        "x": plain("x"), "adj": plain("adj"), "w0": plain("L0_gnn_w"), "w0t": turned("L0_gnn_w"),
        "a12": np.concatenate([inputs["L0_gnn_a1"], inputs["L0_gnn_a2"]], axis=1),
        "wq1": plain("L1_gnn_Wq"), "wk1": plain("L1_gnn_Wk"), "wv1": plain("L1_gnn_Wv"), "wo1": plain("L1_gnn_Wo"),
        "w2": plain("L2_gnn_W"), "w2t": turned("L2_gnn_W"), "a_gat": plain("L2_gnn_a"),
        "wq3": turned("L3_gnn_Wq"), "wk3": turned("L3_gnn_Wk"), "wv3": turned("L3_gnn_Wv"),
        "wg3": turned("L3_gnn_Wg"), "bg": plain("L3_gnn_bg"),
    }
    nc = bacc.Bacc("TRN2", target_bir_lowering=False, num_devices=1)
    args = [nc.dram_tensor("in_" + n, a.shape, mybir.dt.from_np(a.dtype), kind="ExternalInput").ap()
            for n, a in arrays.items()]
    result = nc.dram_tensor("result", (B, N, D), F32, kind="ExternalOutput").ap()
    build(nc, *args, result)
    got = run_bass_kernel_spmd(nc, [{"in_" + n: a for n, a in arrays.items()}], core_ids=[0])
    return got.results[0]["result"]
```

```python
from contextlib import ExitStack

import concourse.bass as bass
from concourse import mybir

F32 = mybir.dt.float32
F32R = mybir.dt.float32r
BF16 = mybir.dt.bfloat16
I32 = mybir.dt.int32
ALU = mybir.AluOpType
ACT = mybir.ActivationFunctionType
AX_X = mybir.AxisListType.X

P = 128
B, N, D = 16, 512, 256
H, DK = 8, 32
NT = N // P
DC = D // P
PAIRS = B // 2
EPS = 1e-5
MASKED = -1e30
BIG = 3.0e38
SCALE = float(DK) ** -0.5
SLOPE0, SLOPE2 = 0.1, 0.2
XW = DK + 1
VISITS = 8
LAG = 3


def layer(v):
    return (v % VISITS) // 2


def graph(v):
    return v % 2



def prepare(v):
    mask = [("mask", v)] if layer(v) == 0 else []
    norm = [("stats", v), ("norm", v), ("ht", v, 0), ("ht", v, 1)]
    if layer(v) == 0:
        return mask + norm + [("s2", v)] + [("v0", v, t) for t in range(NT)]
    if layer(v) == 2:
        return norm + [("rows", v), ("vp", v, 0), ("vp", v, 1), ("cols", v), ("xp", v)]
    return norm + [("qk", v, 0, 0), ("qk", v, 0, 1), ("vp", v, 0), ("vp", v, 1)] \
        + ([("maskt", v, 0), ("maskt", v, 1)] if layer(v) == 1 else [])


def attend(v):
    if layer(v) == 0:
        out = [("emax", v)]
        for t in range(NT + 1):
            if t < NT:
                out.append(("e", v, t))
            if t >= 1:
                out += [("tr", v, t - 1), ("pv0", v, t - 1)]
        return out
    if layer(v) == 2:
        out = [("xa", v, 0), ("bc", v, 0), ("xa", v, 1), ("xb", v, 0), ("xa", v, 2), ("xb", v, 1),
               ("bc", v, 1), ("xa", v, 3), ("xb", v, 2), ("xb", v, 3)]
        out += [("bc", v, 2), ("ms", v, 0), ("ms", v, 1), ("bc", v, 3), ("ms", v, 2), ("ms", v, 3)]
        for h in range(H):
            out.append(("pc", v, h))
            if h + 4 < H:
                out.append(("bc", v, h + 4))
        return out
    out = []
    for n in range(4 * H + LAG):
        if n < 4 * H:
            out.append(("sc", v, n))
        if n >= LAG:
            done = n - LAG
            out.append(("tr", v, done))
            if done % 8 == 1 and done > 8:
                out.append(("pv", v, done // 8 - 1))
            out += {17: [("ri", v, 0)], 19: [("rb", v, 0)], 22: [("no", v, 0)]}.get(done, [])
    return out


def finish(v):
    if layer(v) in (0, 2):
        return ([("z2", v)] if layer(v) == 2 else []) + [("elu", v), ("elu2", v)]
    last = [("ri", v, 1), ("pv", v, 3), ("rb", v, 1), ("no", v, 1)]
    if layer(v) == 1:
        return last + [("y", v, 0), ("y", v, 1)]
    return last + [("cn", v, 0), ("gate", v, 0), ("cn", v, 1), ("gate", v, 1)]


def merge(main, side, start, end):
    out, done = [], 0
    for n, step in enumerate(main):
        while done < len(side) and n >= start + (end - start) * done / len(side):
            out.append(side[done])
            done += 1
        out.append(step)
    return out + side[done:]


def turn():
    out = []
    for v in range(VISITS):
        main = attend(v)
        before = finish(v - 1) if v else []
        ahead = prepare((v + 1) % VISITS)
        if layer(v) in (1, 3):
            half = next(i for i, s in enumerate(main) if s == ("sc", v, 16))
            late = [("qk", v, 1, 0), ("qk", v, 1, 1)]
            first, second = main[:half], main[half:]
            k = next((i for i, s in enumerate(ahead) if s[0] in ("vp", "qk", "s2", "rows")), 0)
            out += merge(first, late + before + ahead[:k], 1, len(first))
            out += merge(second, ahead[k:], 1, len(second) - 1)
        else:
            first = 2 if v == 4 else 0
            out += before[:first] + merge(main, before[first:] + ahead, 1, len(main))
    return out + finish(VISITS - 1)


PROLOGUE = prepare(0)
TURN = turn()
TIMELINE = PROLOGUE + TURN

EVENTS = {
    "mask": ["mask_ready", "adj_used"], "maskt": ["maskt_sums", "maskt_ready"],
    "stats": ["stats_ready", "rstd_ready"], "norm": ["normed"],
    "ht": ["ht_made", "ht_ready"],
    "s2": ["s2_made", "s2_ready"], "v0": ["v_made", "v_ready"], "vp": ["v_made", "v_ready"],
    "qk": ["qk_made", "hi_ready", "lo_ready"],
    "rows": ["rows_made", "rows_ready"], "cols": ["cols_made", "cols_ready"],
    "xp": ["xp_ready"], "xa": ["xhi_ready", "xrest_ready"],
    "xb": ["xmid_ready", "xlo_ready"], "ms": ["ms_made", "ms_ready"],
    "bc": ["bc_made", "edges_ready"], "pc": ["pc_made", "pc_ready", "head_ready"],
    "emax": ["shift_ready"], "e": ["scores_moved", "probs_ready"],
    "sc": ["scores_made", "scores_moved", "probs_ready"],
    "tr": ["probst_made"],
    "pv": ["out_made"], "pv0": ["out_made", "z_ready"],
    "ri": ["rinv_ready"], "rb": ["rb_made", "rb_ready"], "no": ["ot_ready"],
    "y": ["y_made", "x_ready"], "z2": ["z_ready"],
    "elu": ["elu_min", "elu_exp"], "elu2": ["x_ready"],
    "cn": ["cn_made", "cn_used"], "gate": ["gate_made", "tanh_ready", "y_ready"],
}
def mover(step):
    return "act" if step[2] % 8 in (1, 4, 6) else "dve"


def events_of(step):
    own = EVENTS[step[0]]
    if step[0] == "tr":
        own = own + ["probst_by_" + mover(step)]
    return own


AT, PER, AHEAD = {}, {}, {}
for where, steps in (("prologue", PROLOGUE), ("turn", TURN)):
    for step in steps:
        for event in events_of(step):
            if where == "prologue":
                AHEAD[event] = AHEAD.get(event, 0) + 1
            else:
                AT[event, step] = PER.get(event, 0)
                PER[event] = PER.get(event, 0) + 1
CREDIT = dict(PER)

PREPARING = ("mask", "stats", "norm", "ht", "s2", "v0", "rows", "cols", "xp", "vp", "qk", "maskt")
FINISHING = ("ri", "rb", "no", "z2", "elu", "elu2", "y", "cn", "gate")
DELAY = {"dve": {"tr": 1}}


def order(engine, steps):
    def key(n):
        kind, v = steps[n][:2]
        at = n + DELAY.get(engine, {}).get(kind, 0)
        if kind in PREPARING:
            starts = [m for m, s in enumerate(steps) if m > n and s[:2] == attend(v)[0][:2]]
            at = min([at] + [m - 0.5 for m in starts[:1]])
        return at
    return sorted(range(len(steps)), key=key)


MISC = ("ht", "s2", "v0", "vp", "qk", "rows", "cols", "maskt", "ms", "rb", "y", "cn", "gate")
MISC_LAST = {"ht": "ht_ready", "s2": "s2_ready", "v0": "v_ready", "vp": "v_ready", "qk": "lo_ready",
             "rows": "rows_ready", "cols": "cols_ready", "maskt": "maskt_ready", "ms": "ms_ready",
             "rb": "rb_ready", "y": "x_ready", "cn": "cn_used", "gate": "tanh_ready"}
misc_turn = [s for s in TURN if s[0] in MISC]
misc_pro = [s for s in PROLOGUE if s[0] in MISC]
assert len(misc_turn) % 2 == 0


def build(nc, x_in, adj_in, w0, w0t, a12_in, wq1, wk1, wv1, wo1, w2, w2t, a_gat, wq3, wk3, wv3, wg3, bg, out):
    with ExitStack() as ctx:
        def sb(name, shape, dt=F32):
            return ctx.enter_context(nc.sbuf_tensor(name, shape, dt))

        def ps(name, shape, dt=F32):
            return ctx.enter_context(nc.psum_tensor(name, shape, dt))

        def sem(name):
            return ctx.enter_context(nc.semaphore(name))

        x = [sb(f"x{g}", [P, NT, D]) for g in range(2)]
        mask = [sb(f"mask{g}", [P, NT, N], BF16) for g in range(2)]
        edge_t = [sb(f"edge_t{g}", [P, NT, N], BF16) for g in range(2)]
        hn = [sb(f"hn{g}", [P, NT, D]) for g in range(2)]
        ht = [sb(f"ht{g}", [P, DC, N]) for g in range(2)]
        val = [sb(f"val{g}", [P, NT, D + 1]) for g in range(2)]
        s2b = [sb(f"s2b{g}", [P, N]) for g in range(2)]
        rows = s2b
        fa = [sb(f"fa{g}", [P, NT, H]) for g in range(2)]
        fb = [sb(f"fb{g}", [P, NT, H]) for g in range(2)]
        ea = [sb(f"ea{g}", [P, NT, H]) for g in range(2)]
        eb = [sb(f"eb{g}", [P, NT, H]) for g in range(2)]
        sip = [sb(f"sip{g}", [P, NT, H]) for g in range(2)]
        nsj = [sb(f"nsj{g}", [P, NT, H]) for g in range(2)]
        adj = [sb(f"adj{i}", [P, N], I32) for i in range(2)]
        bn = sb("bn", [P, NT, 6])
        mv = sb("mv", [P, NT, 2])
        rstd = sb("rstd", [P, NT])
        vare = sb("vare", [P, NT])
        power = sb("power", [P, NT])
        split = sb("split", [P, 4, N], F32R)
        stack = [sb(f"stack{b}", [96, 2, 4, N], F32R) for b in range(2)]
        moved = [sb(f"moved{i}", [P, N]) for i in range(4)]
        probs = [sb(f"probs{i}", [P, N]) for i in range(4)]
        shift = sb("shift", [P, 4 * H])
        sums = [sb(f"sums{i}", [P, 2, 4, 4]) for i in range(2)]
        rinv = sb("rinv", [P, 4, 4])
        probs_t = [sb(f"probs_t{i}", [P, 4, NT, 2 * P]) for i in range(2)]
        edges = [probs_t[0][:, i, :, :].rearrange("p b c -> p (b c)").bitcast(BF16)
                 .rearrange("p (t n) -> p t n", t=NT) for i in range(4)]
        parts = probs_t[1][:, :, :, :].rearrange("p a b c -> p (a b c)").bitcast(BF16)
        part3 = [parts[:, k * NT * H * 2 * XW:(k + 1) * NT * H * 2 * XW]
                 .rearrange("p (t h c) -> p t h c", t=NT, h=H) for k in range(3)]
        rb = sb("rb", [P, N])
        ot = sb("ot", [P, DC, N])
        vx = sb("vx", [P, NT, H, 2 * XW])
        msum = sb("msum", [P, NT, H, XW])
        part = [sb(f"part{i}", [P, NT, 2 * XW]) for i in range(2)]
        diff = sb("diff", [P, NT, XW])
        numer = sb("numer", [P, NT, H, XW])
        z = sb("z", [P, NT, D])
        ez = sb("ez", [P, NT, D])
        tanh = ez[:, 0:2, :]
        small = sb("small", [P, 4 * NT])
        w_s = {n: sb("w_" + n, [P, DC, D]) for n in ("q1", "k1", "v1", "o1", "2", "q3", "k3", "v3")}
        w0_s = sb("w0_s", [P, DC, D + 1])
        w0_2 = sb("w0_2", [P, DC, P])
        wg_s = sb("wg_s", [P, 4, D])
        wt_s = ez
        a12 = sb("a12", [P, DC, 2])
        adiag = sb("adiag", [P, DC, 40])
        wa = sb("wa", [P, DC, 40])
        bg_s = sb("bg_s", [1, D])
        ident = sb("ident", [P, P])
        ident_b = sb("ident_b", [P, P], BF16)
        ones = sb("ones", [1, P])

        pscore = [ps(f"pscore{i}", [P, N]) for i in range(2)]
        ptrans = [ps(f"ptrans{i}", [P, N]) for i in range(2)]
        pout = [ps(f"pout{i}", [P, N]) for i in range(2)]
        pmisc = [ps(f"pmisc{i}", [P, N]) for i in range(2)]
        pmisc_b = [p[:, :].bitcast(BF16) for p in pmisc]

        S = {e: sem("s_" + e) for e in sorted({e for s in TIMELINE for e in events_of(s)})}
        x_loaded = [sem(f"x_loaded{g}") for g in range(2)]
        adj_loaded = [sem(f"adj_loaded{i}") for i in range(2)]
        out_stored = [sem(f"out_stored{g}") for g in range(2)]
        stacked = [sem(f"stacked{b}") for b in range(2)]
        w_loaded = sem("w_loaded")
        credits = sem("credits")
        carried = sem("carried")
        setup_pool = sem("setup_pool")
        setup_pe = sem("setup_pe")
        setup_dve = sem("setup_dve")
        link_dve = sem("link_dve")
        link_act = sem("link_act")
        link_pool = sem("link_pool")

        class Walk:

            def __init__(self, eng, engine, link=None):
                self.engine = engine
                self.eng, self.link, self.linked, self.i, self.base = eng, link, 0, None, 0

            def at(self, event, step):
                n = AT[event, step] + 1
                if self.i is None:
                    return CREDIT[event] + n - PER[event] + AHEAD[event]
                if TURN_AT[step] > self.place - len(PROLOGUE):
                    n -= PER[event]
                return self.i * PER[event] + CREDIT[event] + AHEAD.get(event, 0) + n

            def next_link(self):
                self.linked += 1
                return (0 if self.i is None else self.i * self.per) + self.base + self.linked

            def run(self, eng_loop, do, per=0):
                self.per = per
                for self.place in order(self.engine, PROLOGUE):
                    do(PROLOGUE[self.place])
                self.base, self.linked = self.linked, 0
                with eng_loop(0, PAIRS) as i:
                    self.i = i
                    for n in order(self.engine, TURN):
                        self.place = len(PROLOGUE) + n
                        do(TURN[n])
                assert self.linked == per, self.linked

        TURN_AT = {s: n for n, s in enumerate(TURN)}

        def misc_bank(w, step):
            seq = misc_pro if w.i is None else misc_turn
            n = seq.index(step)
            return n, n % 2

        def misc_free(w, step):
            n, bank = misc_bank(w, step)
            if w.i is None:
                if n >= 2:
                    w.eng.wait_ge(S[MISC_LAST[misc_pro[n - 2][0]]], w.at(MISC_LAST[misc_pro[n - 2][0]], misc_pro[n - 2]))
            else:
                last = misc_turn[n - 2]
                w.eng.wait_ge(S[MISC_LAST[last[0]]], w.at(MISC_LAST[last[0]], last))
                if n < 2:
                    w.eng.wait_ge(S[MISC_LAST[misc_pro[-1][0]]], w.at(MISC_LAST[misc_pro[-1][0]], misc_pro[-1]))
            return bank

        trs = [s for s in TURN if s[0] == "tr"]
        tr_at = {s: n for n, s in enumerate(trs)}
        scs = [s for s in TURN if s[0] in ("sc", "e")]
        sc_at = {s: n for n, s in enumerate(scs)}
        assert len(trs) % 4 == 0 and len(scs) % 4 == 0 and [s[1:] for s in trs] == [s[1:] for s in scs]
        moves = {s: "probst_by_" + mover(s) for s in trs}
        score_of = {s: ("sc" if layer(s[1]) in (1, 3) else "e",) + s[1:] for s in trs}

        def unpack(n):
            return n // 16, (n // 4) % 4, n % 4

        qks = [s for s in TURN if s[0] == "qk"]
        assert len(qks) % 2 == 0

        def adj_count(w, v, t):
            if w.i is None:
                return CREDIT_ADJ + t + 1
            return w.i * 2 * NT + CREDIT_ADJ + NT + (0 if graph(v) == 1 else NT) + t + 1

        CREDIT_ADJ = 2 * NT

        def last_scores(w, step):
            _, v, b, _ = step
            here = TURN_AT[step]
            mine = [s for s in scs if s[0] == "sc" and unpack(s[2])[0] == b]
            before = [s for s in mine if TURN_AT[s] < here]
            return before[-1] if before else mine[-1]

        def last_of(w, kind, step):
            mine = [s for s in TURN if s[0] == kind]
            before = [s for s in mine if TURN_AT[s] < TURN_AT[step]]
            return before[-1] if before else mine[-1]

        def stacks(w, step):
            _, v, b, _ = step
            same = [s for s in qks if s[2:] == (b, 1)]
            turns = 0 if w.i is None else w.i
            return turns * (16 * 12 * len(same)) + 16 * 12 * (same.index(("qk", v, b, 1)) + 1) + 16

        def split_free(w, eng, step):
            n = qks.index(step)
            last = qks[n - 2]
            back = 16 * 12 * len(qks) // 4 if n < 2 else 0
            eng.wait_ge(stacked[last[2]], stacks(w, last) - back)

        def move_probs_t(w, step, copy):
            _, v, n = step
            bank = tr_at[step] % 2
            w.eng.wait_ge(S["probst_made"], w.at("probst_made", step))
            if layer(v) == 0:
                if v == 0 and n < 2:
                    w.eng.wait_ge(S["out_made"], w.at("out_made", ("pv", 7, 3)))
                elif n >= 2:
                    w.eng.wait_ge(S["out_made"], w.at("out_made", ("pv0", v, n - 2)))
                else:
                    w.eng.wait_ge(S["out_made"], w.at("out_made", ("pv0", 0, n + 2)))
                dst = probs_t[1][:, n % 2, :, 0:P]
                src = ptrans[bank][:, :].rearrange("p (c q) -> p c q", c=NT)
                return copy(dst, src)
            b, t, head = unpack(n)
            buf = (n // 8) % 2
            if n % 8 < 2:
                if n // 8 >= 2:
                    w.eng.wait_ge(S["out_made"], w.at("out_made", ("pv", v, n // 8 - 2)))
                elif v % 2 == 1:
                    w.eng.wait_ge(S["out_made"], w.at("out_made", ("pv", v - 1, n // 8 + 2)))
                elif v == 2:
                    w.eng.wait_ge(S["out_made"], w.at("out_made", ("pv0", 1, 3)))
                else:
                    w.eng.wait_ge(S["pc_made"], w.at("pc_made", ("pc", v - 1, H - 1)))
                    w.eng.wait_ge(S["out_made"], w.at("out_made", ("pv", 3, 3)))
            dst = probs_t[buf][:, head, :, (t % 2) * P:(t % 2 + 1) * P]
            return copy(dst, ptrans[bank][:, :].rearrange("p (c q) -> p c q", c=NT))

        block = ctx.enter_context(nc.Block())

        @block.sync
        def _(sp):
            for name, src in (("q1", wq1), ("k1", wk1), ("v1", wv1), ("o1", wo1), ("2", w2),
                              ("q3", wq3), ("k3", wk3), ("v3", wv3)):
                sp.dma_start(w_s[name][:, :, :], src.rearrange("(c p) n -> p c n", p=P)).then_inc(w_loaded, 16)
            sp.dma_start(w0_s[:, :, 0:D], w0.rearrange("(c p) n -> p c n", p=P)).then_inc(w_loaded, 16)
            sp.dma_start(wg_s[:, :, :], wg3.rearrange("(c p) n -> p c n", p=P)).then_inc(w_loaded, 16)
            sp.dma_start(wt_s[:, 0:2, :], w0t.rearrange("(c p) n -> p c n", p=P)).then_inc(w_loaded, 16)
            sp.dma_start(wt_s[:, 2:4, :], w2t.rearrange("(c p) n -> p c n", p=P)).then_inc(w_loaded, 16)
            sp.dma_start(a12[:, :, :], a12_in.rearrange("(c p) o -> p c o", p=P)).then_inc(w_loaded, 16)
            sp.dma_start(bg_s[:, :], bg.rearrange("(a n) -> a n", a=1)).then_inc(w_loaded, 16)
            sp.wait_ge(setup_pool, 1)
            for h in range(H):
                rows_h = slice(32 * (h % 4), 32 * (h % 4) + 32)
                sp.dma_start(adiag[rows_h, h // 4, h:h + 1],
                             a_gat[h, DK:2 * DK].rearrange("(p o) -> p o", o=1)).then_inc(w_loaded, 16)
                sp.dma_start(adiag[rows_h, h // 4, 32 + h:33 + h],
                             a_gat[h, 0:DK].rearrange("(p o) -> p o", o=1)).then_inc(w_loaded, 16)

            def load_x(index, g):
                sp.dma_start(x[g][:, :, :], x_in[index, :, :].rearrange("(t p) d -> p t d", p=P))\
                    .then_inc(x_loaded[g], 16)

            def do(step):
                kind, v = step[0], step[1]
                g = graph(v)
                if kind == "mask":
                    first = w.i is None
                    index = 0 if first else ((2 * w.i + 2) % B if g == 0 else 2 * w.i + 1)
                    for t in range(NT):
                        sp.wait_ge(S["adj_used"], adj_count(w, v, t - 2))
                        sp.dma_start(adj[t % 2][:, :], adj_in[index, t * P:(t + 1) * P, :])\
                            .then_inc(adj_loaded[t % 2], 16)
                if kind == "qk":
                    _, _, b, which = step
                    if which == 0:
                        return
                    sp.wait_ge(S["hi_ready"], w.at("hi_ready", step))
                    sp.sem_inc(carried, 1)
                    sp.wait_ge(S["lo_ready"], w.at("lo_ready", step))
                    sp.sem_inc(carried, 1)
                    if not (w.i is None):
                        sp.wait_ge(S["scores_made"], w.at("scores_made", last_scores(w, step)))
                    for r, (first, apart) in enumerate(((0, 2), (0, 3), (1, 1))):
                        for head in range(4):
                            rows_h = slice(32 * head, 32 * head + 32)
                            sp.dma_start(stack[b][32 * r:32 * r + 32, :, head, :].bitcast(F32),
                                         split[rows_h, first:first + apart + 1:apart, :].bitcast(F32))\
                                .then_inc(stacked[b], 16)
                if kind == "gate" and step[2] == 1:
                    sp.wait_ge(S["y_ready"], w.at("y_ready", step))
                    where = 2 * w.i + g
                    sp.dma_start(out[where, :, :].rearrange("(t p) d -> p t d", p=P), hn[g][:, :, :])\
                        .then_inc(out_stored[g], 16)
                    load_x((2 * w.i + 2 + g) % B, g)

            load_x(0, 0)
            load_x(1, 1)
            sp.wait_ge(credits, 1)
            w = Walk(sp, "sp")
            w.run(sp.Fori, do)
            for g in range(2):
                sp.wait_ge(out_stored[g], 16 * (PAIRS + 1))
                sp.wait_ge(x_loaded[g], 16 * (PAIRS + 1))

        @block.gpsimd
        def _(pool):
            gp = nc.gpsimd
            for e in S:
                start = CREDIT_ADJ if e == "adj_used" else CREDIT[e]
                pool.sem_inc(S[e], start)
            for s in stacked + out_stored:
                pool.sem_inc(s, 16)
            pool.sem_inc(credits, 1)
            gp.memset(adiag[:, :, :], 0.0).then_inc(setup_pool, 1)
            gp.memset(ident[:, :], 0.0)
            gp.memset(ident_b[:, :], 0.0)
            gp.memset(power[:, :], -0.5)
            gp.memset(ones[:, :], 1.0).then_inc(setup_pool, 1)
            pool.wait_ge(setup_pool, 2)
            gp.affine_select(out=ident[:, :], in_=ident[:, :], compare_op=ALU.not_equal, fill=1.0,
                             base=0, pattern=[[-1, P]], channel_multiplier=1).then_inc(setup_pool, 1)
            gp.affine_select(out=ident_b[:, :], in_=ident_b[:, :], compare_op=ALU.not_equal, fill=1.0,
                             base=0, pattern=[[-1, P]], channel_multiplier=1).then_inc(setup_pool, 1)

            w = Walk(pool, "pool", link_pool)

            def do(step):
                kind, v = step[0], step[1]
                g = graph(v)
                if kind == "stats":
                    pool.wait_ge(S["stats_ready"], w.at("stats_ready", step))
                    pool.sem_inc(carried, 1)
                    gp.tensor_scalar(vare[:, :], mv[:, :, 1], EPS, None, op0=ALU.add).then_inc(link_pool, 1)
                    pool.wait_ge(link_pool, w.next_link())
                    gp.tensor_tensor(rstd[:, :], vare[:, :], power[:, :], ALU.pow)\
                        .then_inc(S["rstd_ready"], 1)
                if kind == "xp":
                    pool.wait_ge(S["v_ready"], w.at("v_ready", ("vp", v, 1)))
                    pool.wait_ge(S["cols_ready"], w.at("cols_ready", ("cols", v)))
                    pool.wait_ge(S["xlo_ready"], w.at("xlo_ready", ("xb", 9 - v, NT - 1)))
                    for t in range(NT):
                        src = val[g][:, t, 0:D].rearrange("p (h d) -> p h d", h=H)
                        for k, f in enumerate((fa, fb)):
                            c0 = k * XW
                            fac = f[g][:, t, :].rearrange("p (h o) -> p h o", o=1).broadcast_to([P, H, DK])
                            gp.tensor_tensor(vx[:, t, :, c0:c0 + DK], src, fac, ALU.mult)
                    for k, f in enumerate((fa, fb)):
                        ins = gp.tensor_copy(vx[:, :, :, k * XW + DK], f[g][:, :, :])
                    ins.then_inc(S["xp_ready"], 1)
                if kind == "xb":
                    t = step[2]
                    pool.wait_ge(S["xmid_ready"], w.at("xmid_ready", step))
                    gp.tensor_tensor(part3[2][:, t, :, :], vx[:, t, :, :], part3[1][:, t, :, :], ALU.subtract)\
                        .then_inc(S["xlo_ready"], 1)
                if kind == "pc":
                    h = step[2]
                    pool.wait_ge(S["pc_ready"], w.at("pc_ready", step))
                    pool.wait_ge(S["head_ready"], w.at("head_ready", last_of(w, "pc", step)))
                    pool.wait_ge(S["ms_ready"], w.at("ms_ready", ("ms", v, NT - 1)))
                    src = part[h % 2]
                    def col(t):
                        return t[g][:, :, h:h + 1].broadcast_to([P, NT, XW])
                    gp.tensor_tensor(diff[:, :, :], msum[:, :, h, :], src[:, :, XW:2 * XW], ALU.subtract).then_inc(link_pool, 1)
                    pool.wait_ge(link_pool, w.next_link())
                    gp.tensor_tensor(diff[:, :, :], diff[:, :, :], col(eb), ALU.mult).then_inc(link_pool, 1)
                    pool.wait_ge(link_pool, w.next_link())
                    gp.tensor_tensor(numer[:, :, h, :], src[:, :, 0:XW], col(ea), ALU.mult).then_inc(link_pool, 1)
                    pool.wait_ge(link_pool, w.next_link())
                    gp.tensor_tensor(numer[:, :, h, :], numer[:, :, h, :], diff[:, :, :], ALU.add)\
                        .then_inc(S["head_ready"], 1)

            w.run(pool.Fori, do, per=sum({"stats": 1, "pc": 3}.get(s[0], 0) for s in TURN))

        @block.scalar
        def _(act):
            sc = nc.scalar
            w = Walk(act, "act", link_act)
            act.wait_ge(credits, 1)

            def do(step):
                kind, v = step[0], step[1]
                g = graph(v)
                bank = misc_bank(w, step)[1] if kind in MISC else None
                if kind == "ht":
                    act.wait_ge(S["ht_made"], w.at("ht_made", step))
                    sc.activation(ht[g][:, step[2], :], pmisc[bank][:, :], ACT.Relu).then_inc(S["ht_ready"], 1)
                if kind == "s2":
                    act.wait_ge(S["s2_made"], w.at("s2_made", step))
                    sc.activation(s2b[g][:, :], pmisc[bank][:, :], ACT.Copy).then_inc(S["s2_ready"], 1)
                if kind == "v0":
                    act.wait_ge(S["v_made"], w.at("v_made", step))
                    sc.activation(val[g][:, step[2], :], pmisc[bank][:, 0:D + 1], ACT.Copy)\
                        .then_inc(S["v_ready"], 1)
                if kind == "vp":
                    j = step[2]
                    act.wait_ge(S["v_made"], w.at("v_made", step))
                    sc.activation(val[g][:, 2 * j:2 * j + 2, 0:D],
                                  pmisc[bank][:, :].rearrange("p (t d) -> p t d", t=2), ACT.Copy)\
                        .then_inc(S["v_ready"], 1)
                if kind == "qk":
                    act.wait_ge(S["qk_made"], w.at("qk_made", step))
                    split_free(w, act, step)
                    sc.activation(split[:, 2 * step[3], :], pmisc[bank][:, :], ACT.Copy).then_inc(S["hi_ready"], 1)
                if kind == "xa":
                    t = step[2]
                    act.wait_ge(S["xp_ready"], w.at("xp_ready", ("xp", v)))
                    event, last_step = ("out_made", ("pv", 3, 3)) if v == 4 else ("pc_made", ("pc", 4, H - 1))
                    act.wait_ge(S[event], w.at(event, last_step))
                    sc.activation(part3[0][:, t, :, :], vx[:, t, :, :], ACT.Copy).then_inc(S["xhi_ready"], 1)
                if kind == "xb":
                    t = step[2]
                    act.wait_ge(S["xrest_ready"], w.at("xrest_ready", ("xa", v, t)))
                    sc.activation(part3[1][:, t, :, :], vx[:, t, :, :], ACT.Copy).then_inc(S["xmid_ready"], 1)
                if kind == "ms":
                    t = step[2]
                    act.wait_ge(S["ms_made"], w.at("ms_made", step))
                    act.wait_ge(S["head_ready"], w.at("head_ready", ("pc", {4: 5, 5: 4}[v], H - 1)))
                    sc.activation(msum[:, t, :, :], pmisc[bank][:, 0:H * XW]
                                  .rearrange("p (h c) -> p h c", h=H), ACT.Copy).then_inc(S["ms_ready"], 1)
                if kind == "cols":
                    act.wait_ge(S["cols_made"], w.at("cols_made", step))
                    pc = pmisc[bank][:, 0:NT * 40].rearrange("p (t c) -> p t c", t=NT)
                    sc.activation(ea[g][:, :, :], pc[:, :, 32:40], ACT.Relu, scale=-1.0).then_inc(link_act, 1)
                    act.wait_ge(link_act, w.next_link())
                    sc.activation(eb[g][:, :, :], pc[:, :, 32:40], ACT.Relu).then_inc(link_act, 1)
                    act.wait_ge(link_act, w.next_link())
                    sc.activation(fa[g][:, :, :], pc[:, :, 0:8], ACT.Exp)
                    sc.activation(fb[g][:, :, :], pc[:, :, 0:8], ACT.Exp, scale=SLOPE2)
                    sc.activation(nsj[g][:, :, :], pc[:, :, 0:8], ACT.Copy, scale=-1.0)
                    sc.activation(sip[g][:, :, :], pc[:, :, 32:40], ACT.Copy)
                    sc.activation(ea[g][:, :, :], ea[g][:, :, :], ACT.Exp, scale=SLOPE2 - 1.0)
                    sc.activation(eb[g][:, :, :], eb[g][:, :, :], ACT.Exp, scale=SLOPE2 - 1.0)\
                        .then_inc(S["cols_ready"], 1)
                if kind == "pc":
                    h = step[2]
                    act.wait_ge(S["pc_made"], w.at("pc_made", step))
                    if h >= 2:
                        act.wait_ge(S["head_ready"], w.at("head_ready", ("pc", v, h - 2)))
                    sc.activation(part[h % 2][:, :, :], ptrans[h % 2][:, 0:NT * 2 * XW]
                                  .rearrange("p (t c) -> p t c", t=NT), ACT.Copy).then_inc(S["pc_ready"], 1)
                if kind == "e":
                    t = step[2]
                    n = sc_at[step]
                    act.wait_ge(S["scores_moved"], w.at("scores_moved", step))
                    if t == 0:
                        act.wait_ge(S["shift_ready"], w.at("shift_ready", ("emax", v)))
                    act.wait_ge(S["z_ready"], w.at("z_ready", ("pv0", 1 - v, t)))
                    probs_free(w, n)
                    sc.activation(probs[n % 4][:, :], moved[n % 4][:, :], ACT.Exp,
                                  bias=small[:, 4 + t:5 + t], accum_out=small[:, 8 + t:9 + t])\
                        .then_inc(S["probs_ready"], 1)
                if kind == "sc":
                    n = sc_at[step]
                    b, t, head = unpack(step[2])
                    act.wait_ge(S["scores_moved"], w.at("scores_moved", step))
                    probs_free(w, n)
                    sc.activation(probs[n % 4][:, :], moved[n % 4][:, :], ACT.Exp, scale=-1.0,
                                  bias=shift[:, step[2]:step[2] + 1],
                                  accum_out=sums[g][:, b, t, head:head + 1]).then_inc(S["probs_ready"], 1)
                if kind == "tr" and mover(step) == "act":
                    move_probs_t(w, step, lambda o, i: sc.activation(o, i, ACT.Copy))\
                        .then_inc(S["probst_by_act"], 1)
                if kind == "rb":
                    act.wait_ge(S["rb_made"], w.at("rb_made", step))
                    sc.activation(rb[:, :], pmisc[bank][:, :], ACT.Copy).then_inc(S["rb_ready"], 1)
                if kind == "elu":
                    act.wait_ge(S["elu_min"], w.at("elu_min", step))
                    sc.activation(ez[:, :, :], ez[:, :, :], ACT.Exp).then_inc(S["elu_exp"], 1)
                if kind == "gate":
                    act.wait_ge(S["gate_made"], w.at("gate_made", step))
                    act.wait_ge(S["y_ready"], w.at("y_ready", last_of(w, "gate", step)))
                    act.wait_ge(S["x_ready"], w.at("x_ready", ("elu2", 5)))
                    sc.activation(tanh, pmisc[bank][:, :].rearrange("p (t d) -> p t d", t=2),
                                  ACT.Tanh, scale=0.5).then_inc(S["tanh_ready"], 1)

            def probs_free(w, n):
                act.wait_ge(S["probst_made"], w.at("probst_made", trs[n - 4]))

            w.run(act.Fori, do, per=sum({"cols": 2}.get(s[0], 0) for s in TURN))

        LINKS = {"stats": 1, "emax": 2, "e": 1, "rows": 2, "elu2": 1, "gate": 1, "z2": 2, "pv0": 1, "ri": 1}

        @block.vector
        def _(dve):
            vec = nc.vector
            w = Walk(dve, "dve", link_dve)
            dve.wait_ge(credits, 1)
            dve.wait_ge(setup_pe, 1)
            vec.tensor_copy(w0_s[:, :, D], pmisc[0][:, 0:4].rearrange("p (c a) -> p c a", c=DC)[:, :, 0])\
                .then_inc(setup_dve, 1)
            for c in range(DC):
                vec.tensor_copy(w0_2[:, c, :], pmisc[0][:, 2 * c + 1:2 * c + 2].broadcast_to([P, P]))\
                    .then_inc(setup_dve, 1)
            vec.tensor_copy(wa[:, :, :], pmisc[0][:, 4:84].rearrange("p (c a) -> p c a", c=DC))\
                .then_inc(setup_dve, 1)

            def do(step):
                kind, v = step[0], step[1]
                g = graph(v)
                L = layer(v)
                bank = misc_bank(w, step)[1] if kind in MISC else None
                turns = 0 if w.i is None else w.i
                if kind == "mask":
                    for t in range(NT):
                        first = w.i is None
                        seen = (t // 2 + 1) if first else turns * 4 + 2 + (0 if g == 1 else 2) + t // 2 + 1
                        dve.wait_ge(adj_loaded[t % 2], 16 * seen)
                        ins = vec.tensor_scalar(mask[g][:, t, :], adj[t % 2][:, :], 0.0, MASKED,
                                                op0=ALU.is_equal, op1=ALU.mult)
                        ins.then_inc(S["adj_used"], 1)
                    w.eng.wait_ge(S["adj_used"], adj_count(w, v, NT - 1))
                    vec.memset(small[:, 15:16], 0.0).then_inc(S["mask_ready"], 1)
                if kind == "maskt":
                    j = step[2]
                    dve.wait_ge(S["maskt_sums"], w.at("maskt_sums", step))
                    vec.tensor_scalar(edge_t[g][:, 2 * j:2 * j + 2, :],
                                      pmisc_b[bank].rearrange("p (t n) -> p t n", t=2),
                                      0.0, None, op0=ALU.is_equal).then_inc(S["maskt_ready"], 1)
                if kind == "stats":
                    if L == 0:
                        dve.wait_ge(x_loaded[g], 16 if w.i is None else (w.i + (2 if g == 0 else 1)) * 16)
                    else:
                        dve.wait_ge(S["x_ready"], w.at("x_ready", ("y", v - 2, 1) if L == 2 else ("elu2", v - 2)))
                    dve.wait_ge(S["rstd_ready"], w.at("rstd_ready", last_of(w, "stats", step))) if w.i is not None else None
                    dve.wait_ge(S["normed"], w.at("normed", last_of(w, "norm", step))) if w.i is not None else None
                    for t in range(NT):
                        ins = vec.bn_stats(bn[:, t, :], x[g][:, t, :])
                    ins.then_inc(link_dve, 1)
                    dve.wait_ge(link_dve, w.next_link())
                    dve.sem_inc(carried, 1)
                    for t in range(NT):
                        ins = vec.bn_aggr(mv[:, t, :], bn[:, t, :])
                    ins.then_inc(S["stats_ready"], 1)
                if kind == "norm":
                    dve.wait_ge(S["rstd_ready"], w.at("rstd_ready", ("stats", v)))
                    if L == 0:
                        if w.i is not None:
                            dve.wait_ge(out_stored[g], 16 * (w.i + (2 if g == 0 else 1)))
                    for t in range(NT):
                        ins = vec.tensor_scalar(hn[g][:, t, :], x[g][:, t, :], mv[:, t, 0:1], rstd[:, t:t + 1],
                                                op0=ALU.subtract, op1=ALU.mult)
                    ins.then_inc(S["normed"], 1)
                if kind == "qk":
                    split_free(w, dve, step)
                    dve.wait_ge(S["hi_ready"], w.at("hi_ready", step))
                    vec.tensor_tensor(split[:, 2 * step[3] + 1, :], pmisc[bank][:, :],
                                      split[:, 2 * step[3], :].bitcast(F32), ALU.subtract)\
                        .then_inc(S["lo_ready"], 1)
                if kind == "rows":
                    dve.wait_ge(S["rows_made"], w.at("rows_made", step))
                    pr = pmisc[bank]
                    vec.tensor_reduce(small[0:8, 12:13], pr[0:8, :], axis=AX_X, op=ALU.max)
                    vec.tensor_reduce(small[32:40, 12:13], pr[0:8, :], axis=AX_X, op=ALU.max).then_inc(link_dve, 1)
                    dve.wait_ge(link_dve, w.next_link())
                    vec.tensor_scalar(rows[g][0:8, :], pr[0:8, :], small[0:8, 12:13], None,
                                              op0=ALU.subtract).then_inc(link_dve, 1)
                    dve.wait_ge(link_dve, w.next_link())
                    vec.tensor_scalar(rows[g][32:40, :], pr[32:40, :], small[32:40, 12:13], None,
                                      op0=ALU.add).then_inc(S["rows_ready"], 1)
                if kind == "emax":
                    dve.wait_ge(S["s2_ready"], w.at("s2_ready", ("s2", v)))
                    dve.wait_ge(S["v_ready"], w.at("v_ready", ("v0", v, NT - 1)))
                    dve.wait_ge(S["mask_ready"], w.at("mask_ready", ("mask", v)))
                    for t in range(NT):
                        first = scs[(sc_at[("e", v, 0)] + t) - 4]
                        dve.wait_ge(S["probs_ready"], w.at("probs_ready", first))
                        dve.sem_inc(carried, 1)
                        ins = vec.tensor_tensor_reduce(out=moved[(sc_at[("e", v, 0)] + t) % 4][:, :],
                                                       in0=s2b[g][:, :], in1=mask[g][:, t, :], scale=1.0,
                                                       scalar=-BIG, op0=ALU.add, op1=ALU.max,
                                                       accum_out=small[:, t:t + 1])
                    ins.then_inc(link_dve, 1)
                    dve.wait_ge(link_dve, w.next_link())
                    s1 = val[g][:, :, D]
                    vec.scalar_tensor_tensor(out=small[:, 0:4], in0=small[:, 0:4], scalar=-1.0,
                                                     in1=s1, op0=ALU.mult, op1=ALU.subtract).then_inc(link_dve, 1)
                    dve.wait_ge(link_dve, w.next_link())
                    vec.scalar_tensor_tensor(out=small[:, 4:8], in0=small[:, 0:4], scalar=SLOPE0,
                                             in1=small[:, 0:4], op0=ALU.mult, op1=ALU.min)\
                        .then_inc(S["shift_ready"], 1)
                if kind == "e":
                    t = step[2]
                    buf = moved[sc_at[step] % 4]
                    vec.tensor_scalar(buf[:, :], buf[:, :], val[g][:, t, D:D + 1], None, op0=ALU.add).then_inc(link_dve, 1)
                    dve.wait_ge(link_dve, w.next_link())
                    vec.scalar_tensor_tensor(out=buf[:, :], in0=buf[:, :], scalar=SLOPE0, in1=buf[:, :],
                                             op0=ALU.mult, op1=ALU.max).then_inc(S["scores_moved"], 1)
                if kind == "sc":
                    n = sc_at[step]
                    b, t, head = unpack(step[2])
                    if step[2] == 0:
                        dve.wait_ge(S["mask_ready"], w.at("mask_ready", ("mask", g)))
                    dve.wait_ge(S["probs_ready"], w.at("probs_ready", scs[n - 4]))
                    dve.wait_ge(S["scores_made"], w.at("scores_made", step))
                    dve.sem_inc(carried, 1)
                    vec.tensor_tensor_reduce(out=moved[n % 4][:, :], in0=pscore[n % 2][:, :],
                                             in1=mask[g][:, t, :], scale=-SCALE, scalar=BIG,
                                             op0=ALU.add, op1=ALU.min,
                                             accum_out=shift[:, step[2]:step[2] + 1])\
                        .then_inc(S["scores_moved"], 1)
                if kind == "tr" and mover(step) == "dve":
                    move_probs_t(w, step, vec.tensor_copy).then_inc(S["probst_by_dve"], 1)
                if kind == "ri":
                    b = step[2]
                    dve.wait_ge(S["probs_ready"], w.at("probs_ready", ("sc", v, 16 * b + 15)))
                    vec.reciprocal(rinv[:, :, :], sums[g][:, b, :, :]).then_inc(link_dve, 1)
                    dve.wait_ge(link_dve, w.next_link())
                    rep = rinv[:, :, :].rearrange("p t (h o) -> p (t h) o", o=1).broadcast_to([P, 16, DK])
                    vec.tensor_copy(rb[:, :].rearrange("p (a d) -> p a d", d=DK), rep)\
                        .then_inc(S["rinv_ready"], 1)
                if kind == "no":
                    b = step[2]
                    dve.wait_ge(S["out_made"], w.at("out_made", ("pv", v, 2 * b + 1)))
                    dve.wait_ge(S["rb_ready"], w.at("rb_ready", ("rb", v, b)))
                    last = v - 1 if v % 2 == 1 else {2: 7, 6: 3}[v]
                    event, last_step = ("gate_made", ("gate", last, 1)) if layer(last) == 3 else ("y_made", ("y", last, 1))
                    dve.wait_ge(S[event], w.at(event, last_step))
                    if L == 1:
                        ins = vec.scalar_tensor_tensor(out=ot[:, b, :], in0=pout[b][:, :], scalar=0.0,
                                                       in1=rb[:, :], op0=ALU.max, op1=ALU.mult)
                    else:
                        ins = vec.tensor_tensor(ot[:, b, :], pout[b][:, :], rb[:, :], ALU.mult)
                    ins.then_inc(S["ot_ready"], 1)
                if kind == "y":
                    j = step[2]
                    dve.wait_ge(S["y_made"], w.at("y_made", step))
                    half = x[g][:, 2 * j:2 * j + 2, :]
                    vec.tensor_tensor(half, pmisc[bank][:, :].rearrange("p (t d) -> p t d", t=2), half, ALU.add)\
                        .then_inc(S["x_ready"], 1)
                if kind == "pv0":
                    t = step[2]
                    dve.wait_ge(S["out_made"], w.at("out_made", step))
                    dve.wait_ge(S["probs_ready"], w.at("probs_ready", ("e", v, t)))
                    vec.reciprocal(small[:, 13:14], small[:, 8 + t:9 + t]).then_inc(link_dve, 1)
                    dve.wait_ge(link_dve, w.next_link())
                    vec.tensor_scalar(z[:, t, :], pout[t % 2][:, 0:D], small[:, 13:14], None, op0=ALU.mult)\
                        .then_inc(S["z_ready"], 1)
                if kind == "xa":
                    t = step[2]
                    dve.wait_ge(S["xhi_ready"], w.at("xhi_ready", step))
                    vec.tensor_tensor(vx[:, t, :, :], vx[:, t, :, :], part3[0][:, t, :, :], ALU.subtract)\
                        .then_inc(S["xrest_ready"], 1)
                if kind == "bc":
                    h = step[2]
                    dst = edges[h % 4]
                    dve.wait_ge(S["bc_made"], w.at("bc_made", step))
                    if h == 0:
                        dve.wait_ge(S["maskt_ready"], w.at("maskt_ready", ("maskt", 2 + g, 1)))
                    if h >= 4:
                        dve.wait_ge(S["pc_made"], w.at("pc_made", ("pc", v, h - 4)))
                    elif v == 5:
                        dve.wait_ge(S["pc_made"], w.at("pc_made", ("pc", 4, h + 4)))
                    else:
                        dve.wait_ge(S["out_made"], w.at("out_made", ("pv", 3, 2)))
                    for t in range(NT):
                        ins = vec.scalar_tensor_tensor(out=dst[:, t, :], in0=pscore[h % 2][:, :],
                                                       scalar=nsj[g][:, t, h:h + 1], in1=edge_t[g][:, t, :],
                                                       op0=ALU.is_gt, op1=ALU.mult)
                    ins.then_inc(S["edges_ready"], 1)
                if kind == "z2":
                    dve.wait_ge(S["head_ready"], w.at("head_ready", ("pc", v, H - 1)))
                    den = ez[:, 0, 0:NT * H].rearrange("p (t h) -> p t h", t=NT)
                    dve.wait_ge(S["elu_exp"], w.at("elu_exp", last_of(w, "elu", ("elu", v))))
                    dve.wait_ge(S["x_ready"], w.at("x_ready", ("elu2", v - 1) if v == 5 else ("elu2", 1)))
                    vec.tensor_scalar(den, numer[:, :, :, DK], 1e-37, None, op0=ALU.max).then_inc(link_dve, 1)
                    dve.wait_ge(link_dve, w.next_link())
                    vec.reciprocal(den, den).then_inc(link_dve, 1)
                    dve.wait_ge(link_dve, w.next_link())
                    for t in range(NT):
                        fac = den[:, t, :].rearrange("p (h o) -> p h o", o=1).broadcast_to([P, H, DK])
                        ins = vec.tensor_tensor(z[:, t, :].rearrange("p (h d) -> p h d", h=H),
                                                numer[:, t, :, 0:DK], fac, ALU.mult)
                    ins.then_inc(S["z_ready"], 1)
                if kind == "elu":
                    dve.wait_ge(S["z_ready"], w.at("z_ready", ("z2", v) if L == 2 else ("pv0", v, NT - 1)))
                    dve.wait_ge(S["tanh_ready"], w.at("tanh_ready", ("gate", 7, 1)))
                    vec.tensor_scalar(ez[:, :, :], z[:, :, :], 0.0, None, op0=ALU.min).then_inc(S["elu_min"], 1)
                if kind == "elu2":
                    dve.wait_ge(S["elu_exp"], w.at("elu_exp", ("elu", v)))
                    vec.scalar_tensor_tensor(out=x[g][:, :, :], in0=ez[:, :, :], scalar=-1.0,
                                                     in1=x[g][:, :, :], op0=ALU.add, op1=ALU.add).then_inc(link_dve, 1)
                    dve.wait_ge(link_dve, w.next_link())
                    vec.scalar_tensor_tensor(out=x[g][:, :, :], in0=z[:, :, :], scalar=0.0,
                                             in1=x[g][:, :, :], op0=ALU.max, op1=ALU.add)\
                        .then_inc(S["x_ready"], 1)
                if kind == "cn":
                    j = step[2]
                    dve.wait_ge(S["cn_made"], w.at("cn_made", step))
                    c = pmisc[bank][:, :].rearrange("p (t d) -> p t d", t=2)
                    sl = slice(2 * j, 2 * j + 2)
                    vec.scalar_tensor_tensor(out=hn[g][:, sl, :], in0=hn[g][:, sl, :], scalar=0.0, in1=c,
                                             op0=ALU.max, op1=ALU.subtract)
                    vec.tensor_tensor(x[g][:, sl, :], c, x[g][:, sl, :], ALU.add).then_inc(S["cn_used"], 1)
                if kind == "gate":
                    j = step[2]
                    dve.wait_ge(S["tanh_ready"], w.at("tanh_ready", step))
                    dve.wait_ge(S["cn_used"], w.at("cn_used", ("cn", v, j)))
                    sl = slice(2 * j, 2 * j + 2)
                    vec.scalar_tensor_tensor(out=hn[g][:, sl, :], in0=tanh, scalar=1.0,
                                                     in1=hn[g][:, sl, :], op0=ALU.add, op1=ALU.mult).then_inc(link_dve, 1)
                    dve.wait_ge(link_dve, w.next_link())
                    vec.scalar_tensor_tensor(out=hn[g][:, sl, :], in0=hn[g][:, sl, :], scalar=0.5,
                                             in1=x[g][:, sl, :], op0=ALU.mult, op1=ALU.add)\
                        .then_inc(S["y_ready"], 1)

            w.run(dve.Fori, do, per=sum(LINKS.get(s[0], 0) for s in TURN))

        @block.tensor
        def _(pe):
            mm = nc.tensor.matmul
            w = Walk(pe, "pe")
            pe.wait_ge(w_loaded, 16 * (14 + 2 * H))
            pe.wait_ge(credits, 1)
            for c in range(DC):
                for o in range(DC):
                    mm(pmisc[0][:, 2 * c:2 * c + 2], wt_s[:, o, P * c:P * c + P], a12[:, o, :],
                       start=o == 0, stop=o == DC - 1)
            for c in range(DC):
                for o in range(DC):
                    last = mm(pmisc[0][:, 4 + 40 * c:44 + 40 * c], wt_s[:, 2 + o, P * c:P * c + P],
                              adiag[:, o, :], start=o == 0, stop=o == DC - 1)
            last.then_inc(setup_pe, 1)
            pe.wait_ge(setup_dve, 4)
            pe.wait_ge(setup_pool, 4)

            def do(step):
                kind, v = step[0], step[1]
                g = graph(v)
                L = layer(v)
                bank = misc_free(w, step) if kind in MISC else None
                if kind == "ht":
                    j = step[2]
                    pe.wait_ge(S["normed"], w.at("normed", ("norm", v)))
                    for t in range(NT):
                        last = nc.tensor.transpose(pmisc[bank][:, P * t:P * t + P],
                                                   hn[g][:, t, P * j:P * j + P], ident[:, :])
                    last.then_inc(S["ht_made"], 1)
                if kind in ("s2", "v0", "vp", "rows", "qk"):
                    pe.wait_ge(S["ht_ready"], w.at("ht_ready", ("ht", v, 1)))
                if kind == "s2":
                    for c in range(DC):
                        last = mm(pmisc[bank][:, :], w0_2[:, c, :], ht[g][:, c, :], start=c == 0, stop=c == DC - 1)
                    last.then_inc(S["s2_made"], 1)
                if kind == "v0":
                    t = step[2]
                    for c in range(DC):
                        last = mm(pmisc[bank][:, 0:D + 1], ht[g][:, c, P * t:P * t + P], w0_s[:, c, :],
                                  start=c == 0, stop=c == DC - 1)
                    last.then_inc(S["v_made"], 1)
                if kind == "vp":
                    wv = w_s[{1: "v1", 2: "2", 3: "v3"}[L]]
                    for k in range(2):
                        t = 2 * step[2] + k
                        for c in range(DC):
                            last = mm(pmisc[bank][:, D * k:D * k + D], ht[g][:, c, P * t:P * t + P], wv[:, c, :],
                                      start=c == 0, stop=c == DC - 1)
                    last.then_inc(S["v_made"], 1)
                if kind == "qk":
                    _, _, b, which = step
                    wp = w_s["qk"[which] + str(L)]
                    for c in range(DC):
                        last = mm(pmisc[bank][:, :], wp[:, c, P * b:P * b + P], ht[g][:, c, :],
                                  start=c == 0, stop=c == DC - 1)
                    last.then_inc(S["qk_made"], 1)
                if kind == "rows":
                    for c in range(DC):
                        last = mm(pmisc[bank][0:40, :], wa[:, c, :], ht[g][:, c, :], start=c == 0, stop=c == DC - 1)
                    last.then_inc(S["rows_made"], 1)
                if kind == "cols":
                    pe.wait_ge(S["rows_ready"], w.at("rows_ready", ("rows", v)))
                    pe.sem_inc(carried, 1)
                    for t in range(NT):
                        last = nc.tensor.transpose(pmisc[bank][:, 40 * t:40 * t + 40],
                                                   rows[g][0:40, P * t:P * t + P], ident[0:40, 0:40])
                    last.then_inc(S["cols_made"], 1)
                if kind == "maskt":
                    j = step[2]
                    pe.wait_ge(S["mask_ready"], w.at("mask_ready", ("mask", g)))
                    for k in range(2):
                        for t in range(NT):
                            key = 2 * j + k
                            last = nc.tensor.transpose(pmisc_b[bank][:, N * k + P * t:N * k + P * t + P],
                                                       mask[g][:, t, P * key:P * key + P], ident_b[:, :])
                    last.then_inc(S["maskt_sums"], 1)
                if kind == "sc":
                    n = sc_at[step]
                    b, t, head = unpack(step[2])
                    if step[2] % 16 == 0:
                        pe.wait_ge(stacked[b], stacks(w, ("qk", v, b, 1)))
                    if step[2] >= 2:
                        pe.wait_ge(S["scores_moved"], w.at("scores_moved", ("sc", v, step[2] - 2)))
                    elif v % 2 == 1:
                        pe.wait_ge(S["scores_moved"], w.at("scores_moved", ("sc", v - 1, 30 + step[2])))
                    else:
                        pe.wait_ge(S["scores_moved"], w.at("scores_moved", ("sc", {2: 7, 6: 3}[v], 30 + step[2])))
                        pe.wait_ge(S["edges_ready"], w.at("edges_ready", ("bc", 5, 6 + step[2])))
                    mm(pscore[n % 2][:, :], stack[b][:, 0, head, P * t:P * t + P], stack[b][:, 1, head, :],
                       start=True, stop=True).then_inc(S["scores_made"], 1)
                if kind == "tr":
                    at = tr_at[step]
                    pe.wait_ge(S["probs_ready"], w.at("probs_ready", score_of[step]))
                    last_tr = trs[at - 2]
                    pe.wait_ge(S[moves[last_tr]], w.at(moves[last_tr], last_tr))
                    pe.wait_ge(S["pc_ready"], w.at("pc_ready", ("pc", 5, H - 2 + at % 2)))
                    for c in range(NT):
                        last = nc.tensor.transpose(ptrans[at % 2][:, P * c:P * c + P],
                                                   probs[sc_at[score_of[step]] % 4][:, P * c:P * c + P],
                                                   ident[:, :])
                    last.then_inc(S["probst_made"], 1)
                if kind == "pv0":
                    t = step[2]
                    pe.wait_ge(S[moves["tr", v, t]], w.at(moves["tr", v, t], ("tr", v, t)))
                    pe.wait_ge(S["v_ready"], w.at("v_ready", ("v0", v, NT - 1)))
                    pe.wait_ge(S["ot_ready"], w.at("ot_ready", ("no", 7, t % 2)))
                    if t >= 2:
                        pe.wait_ge(S["z_ready"], w.at("z_ready", ("pv0", v, t - 2)))
                    elif v == 1:
                        pe.wait_ge(S["z_ready"], w.at("z_ready", ("pv0", 0, t + 2)))
                    for c in range(NT):
                        last = mm(pout[t % 2][:, 0:D], probs_t[1][:, t % 2, c, 0:P], val[g][:, c, 0:D],
                                  start=c == 0, stop=c == NT - 1)
                    last.then_inc(S["out_made"], 1)
                if kind == "pv":
                    quarter = step[2]
                    b, half = quarter // 2, quarter % 2
                    mine = [s for s in trs if s[1] == v and s[2] // 8 == quarter]
                    for last in {moves[s]: s for s in mine}.values():
                        pe.wait_ge(S[moves[last]], w.at(moves[last], last))
                    pe.wait_ge(S["v_ready"], w.at("v_ready", ("vp", v, 1)))
                    if half == 0:
                        if v % 2 == 1:
                            pe.wait_ge(S["ot_ready"], w.at("ot_ready", ("no", v - 1, b)))
                        else:
                            pe.wait_ge(S["ot_ready"], w.at("ot_ready", ("no", {2: 7, 6: 3}[v], b)))
                            pe.wait_ge(S["z_ready"], w.at("z_ready", ("pv0", 1, 2 + b)))
                    for c in range(NT):
                        for head in range(4):
                            col = DK * (4 * b + head)
                            last = mm(pout[b][32 * head:32 * head + 32, 2 * P * half:2 * P * (half + 1)],
                                      val[g][:, c, col:col + DK], probs_t[quarter % 2][:, head, c, :],
                                      start=c == 0, stop=c == NT - 1, skip_group_check=True)
                    last.then_inc(S["out_made"], 1)
                if kind == "rb":
                    pe.wait_ge(S["rinv_ready"], w.at("rinv_ready", ("ri", *step[1:])))
                    for t in range(NT):
                        last = nc.tensor.transpose(pmisc[bank][:, P * t:P * t + P], rb[:, P * t:P * t + P],
                                                   ident[:, :])
                    last.then_inc(S["rb_made"], 1)
                if kind == "y":
                    pe.wait_ge(S["ot_ready"], w.at("ot_ready", ("no", v, 1)))
                    for k in range(2):
                        t = 2 * step[2] + k
                        for c in range(DC):
                            last = mm(pmisc[bank][:, D * k:D * k + D], ot[:, c, P * t:P * t + P],
                                      w_s["o1"][:, c, :], start=c == 0, stop=c == DC - 1)
                    last.then_inc(S["y_made"], 1)
                if kind == "cn":
                    pe.wait_ge(S["ot_ready"], w.at("ot_ready", ("no", v, 1)))
                    for k in range(2):
                        t = 2 * step[2] + k
                        for c in range(DC):
                            at = D * k + P * c
                            last = nc.tensor.transpose(pmisc[bank][:, at:at + P], ot[:, c, P * t:P * t + P],
                                                       ident[:, :])
                    last.then_inc(S["cn_made"], 1)
                if kind == "gate":
                    pe.wait_ge(S["ot_ready"], w.at("ot_ready", ("no", v, 1)))
                    for k in range(2):
                        t = 2 * step[2] + k
                        dst = pmisc[bank][:, D * k:D * k + D]
                        mm(dst, ones[0:1, :], bg_s[0:1, :], start=True, stop=False)
                        for c in range(4):
                            src = ot[:, c, P * t:P * t + P] if c < 2 else ht[g][:, c - 2, P * t:P * t + P]
                            last = mm(dst, src, wg_s[:, c, :], start=False, stop=c == 3)
                    last.then_inc(S["gate_made"], 1)
                if kind == "ms":
                    t = step[2]
                    pe.wait_ge(S["maskt_ready"], w.at("maskt_ready", ("maskt", 2 + g, 1)))
                    pe.wait_ge(S["xlo_ready"], w.at("xlo_ready", ("xb", v, NT - 1)))
                    for n in range(3 * NT):
                        c, k = divmod(n, 3)
                        last = mm(pmisc[bank][:, 0:H * XW], edge_t[g][:, c, P * t:P * t + P],
                                  part3[k][:, c, :, XW:2 * XW], start=n == 0, stop=n == 3 * NT - 1)
                    last.then_inc(S["ms_made"], 1)
                if kind == "bc":
                    h = step[2]
                    pe.wait_ge(S["cols_ready"], w.at("cols_ready", ("cols", v)))
                    if h >= 2:
                        pe.wait_ge(S["edges_ready"], w.at("edges_ready", ("bc", v, h - 2)))
                    elif v == 5:
                        pe.wait_ge(S["edges_ready"], w.at("edges_ready", ("bc", 4, 6 + h)))
                    else:
                        pe.wait_ge(S["scores_moved"], w.at("scores_moved", ("sc", 3, 30 + h)))
                    for t in range(NT):
                        last = nc.tensor.transpose(pscore[h % 2][:, P * t:P * t + P],
                                                   sip[g][:, t, h:h + 1].broadcast_to([P, P]), ident[:, :])
                    last.then_inc(S["bc_made"], 1)
                if kind == "pc":
                    h = step[2]
                    pe.wait_ge(S["edges_ready"], w.at("edges_ready", ("bc", v, h)))
                    if h >= 2:
                        pe.wait_ge(S["pc_ready"], w.at("pc_ready", ("pc", v, h - 2)))
                    elif v == 5:
                        pe.wait_ge(S["pc_ready"], w.at("pc_ready", ("pc", 4, 6 + h)))
                    else:
                        pe.wait_ge(S[moves["tr", 3, 30 + h]], w.at(moves["tr", 3, 30 + h], ("tr", 3, 30 + h)))
                    pe.wait_ge(S["xlo_ready"], w.at("xlo_ready", ("xb", v, NT - 1)))
                    for t in range(NT):
                        for n in range(3 * NT):
                            c, k = divmod(n, 3)
                            last = mm(ptrans[h % 2][:, 2 * XW * t:2 * XW * (t + 1)],
                                      edges[h % 4][:, c, P * t:P * t + P], part3[k][:, c, h, :],
                                      start=n == 0, stop=n == 3 * NT - 1)
                    last.then_inc(S["pc_made"], 1)

            w.run(pe.Fori, do)



def kernel(**inputs):
    import numpy as np
    import concourse.bacc as bacc
    from concourse.bass_utils import run_bass_kernel_spmd

    plain = lambda name: np.ascontiguousarray(inputs[name])
    turned = lambda name: np.ascontiguousarray(np.asarray(inputs[name]).T)
    arrays = {
        "x": plain("x"), "adj": plain("adj"), "w0": plain("L0_gnn_w"), "w0t": turned("L0_gnn_w"),
        "a12": np.concatenate([inputs["L0_gnn_a1"], inputs["L0_gnn_a2"]], axis=1),
        "wq1": plain("L1_gnn_Wq"), "wk1": plain("L1_gnn_Wk"), "wv1": plain("L1_gnn_Wv"), "wo1": plain("L1_gnn_Wo"),
        "w2": plain("L2_gnn_W"), "w2t": turned("L2_gnn_W"), "a_gat": plain("L2_gnn_a"),
        "wq3": turned("L3_gnn_Wq"), "wk3": turned("L3_gnn_Wk"), "wv3": turned("L3_gnn_Wv"),
        "wg3": turned("L3_gnn_Wg"), "bg": plain("L3_gnn_bg"),
    }
    nc = bacc.Bacc("TRN2", target_bir_lowering=False, num_devices=1)
    args = [nc.dram_tensor("in_" + n, a.shape, mybir.dt.from_np(a.dtype), kind="ExternalInput").ap()
            for n, a in arrays.items()]
    result = nc.dram_tensor("result", (B, N, D), F32, kind="ExternalOutput").ap()
    build(nc, *args, result)
    got = run_bass_kernel_spmd(nc, [{"in_" + n: a for n, a in arrays.items()}], core_ids=[0])
    return got.results[0]["result"]
```

```python
from contextlib import ExitStack

import concourse.bass as bass
from concourse import mybir

F32 = mybir.dt.float32
F32R = mybir.dt.float32r
BF16 = mybir.dt.bfloat16
I32 = mybir.dt.int32
ALU = mybir.AluOpType
ACT = mybir.ActivationFunctionType
AX_X = mybir.AxisListType.X

P = 128
B, N, D = 16, 512, 256
H, DK = 8, 32
NT = N // P
DC = D // P
PAIRS = B // 2
EPS = 1e-5
MASKED = -1e30
BIG = 3.0e38
SCALE = float(DK) ** -0.5
SLOPE0, SLOPE2 = 0.1, 0.2
XW = DK + 1
VISITS = 8
RING = 8
LAG = 4


def layer(v):
    return (v % VISITS) // 2


def graph(v):
    return v % 2



def prepare(v):
    norm = [("stats", v), ("norm", v), ("ht", v, 0), ("ht", v, 1)]
    if layer(v) == 0:
        return [("mask", v)] + norm + [("s2", v)] + [("v0", v, t) for t in range(NT)]
    if layer(v) == 2:
        return norm + [("rows", v), ("vp", v, 0), ("vp", v, 1), ("cols", v), ("xp", v),
                       ("maskt", v, 0), ("maskt", v, 1)]
    return norm + [("qk", v, 0, 0), ("qk", v, 0, 1), ("vp", v, 0), ("vp", v, 1)]


def attend(v, guests=()):
    if layer(v) == 2:
        out = [(part, v, t) for part in ("xa", "xb") for t in range(NT)]
        out += [("bc", v, 0), ("bc", v, 1), ("bc", v, 2), ("ms", v, 0), ("ms", v, 1), ("bc", v, 3),
                ("ms", v, 2), ("ms", v, 3)]
        for h in range(H):
            out.append(("pc", v, h))
            if h + 4 < H:
                out.append(("bc", v, h + 4))
        return out
    scores = [("sc", v, n) for n in range(4 * H)]
    for t, place in enumerate(guests):
        scores.insert(place, ("e", {7: 0, 2: 1}[v], t))
    early = LAG if v != 6 else 0
    then = {6: 7, 7: 2, 2: 3}.get(v)
    out, ready = [], []
    for n in range(early, len(scores) + LAG):
        if n < len(scores):
            out.append(scores[n])
        elif then:
            out.append(("sc", then, n - len(scores)))
        if n >= LAG:
            kind, u, done = scores[n - LAG]
            out += [("tr", u, done)] + ready
            ready = []
            if kind == "e":
                ready = [("pv0", u, done)]
            else:
                if done % 8 == 1 and done > 8:
                    out.append(("pv", v, done // 8 - 1))
                out += {17: [("ri", v, 0)], 19: [("rb", v, 0)], 22: [("no", v, 0)]}.get(done, [])
    return out


def finish(v):
    if layer(v) in (0, 2):
        return ([("z2", v)] if layer(v) == 2 else []) + [("elu", v), ("elu2", v)]
    last = [("ri", v, 1), ("pv", v, 3), ("rb", v, 1), ("no", v, 1)]
    if layer(v) == 1:
        return last + [("y", v, 0), ("y", v, 1)]
    return last + [("cn", v, 0), ("gate", v, 0), ("cn", v, 1), ("gate", v, 1)]


def merge(main, side, start, end):
    out, done = [], 0
    for n, step in enumerate(main):
        while done < len(side) and n >= start + (end - start) * done / len(side):
            out.append(side[done])
            done += 1
        out.append(step)
    return [s for s in out + side[done:] if s is not None]


def cut(steps, at):
    places = [0] + [steps.index(s) for s in at] + [len(steps)]
    return [steps[a:b] for a, b in zip(places, places[1:])]


GUESTS = (7, 10, 11, 12)
SPREAD = {4: (8, 22), 5: (8, 26), "3a": (0, 25), "3b": (8, 61), "6a": (0, 27), "6b": (1, 37),
          "7a": (0, 6), "7b": (1, 28), "7c": (0, 43), "2a": (3, 5), "2b": (2, 28), "2c": (0, 33)}


def visit(v):
    main, before = attend(v, GUESTS if v in (2, 7) else ()), finish({2: 7}.get(v, v - 1))
    if layer(v) == 2:
        first = 2 if v == 4 else 0
        return before[:first] + merge(main, before[first:] + prepare(v + 1), *SPREAD[v])
    qk2, qk3 = [("qk", v, 1, 0), ("qk", v, 1, 1)]
    if v == 3:
        first, second = cut(main, [("sc", v, 16)])
        ahead = prepare(4)
        return merge(first, before[:2] + [None, qk2, qk3] + before[2:] + ahead[:4], *SPREAD["3a"]) \
            + merge(second, ahead[4:], *SPREAD["3b"])
    then = {6: 7, 7: 2, 2: 3}[v]
    stats, norm, ht0, ht1, qk0, qk1, vp0, vp1 = prepare(then)
    if v == 6:
        first, second = cut(main, [("sc", v, 16)])
        stats0, norm0, ht2, ht3, s2 = prepare(0)[1:6]
        z2, elu, elu2 = before
        side = [None, None, z2, elu, None, elu2, qk2, stats, qk3, norm, None, ht0, stats0, ht1, norm0]
        return merge(first, side, *SPREAD["6a"]) \
            + merge(second, [ht2, ht3, qk0, s2, qk1, vp0, vp1, None], *SPREAD["6b"])
    g = {7: 0, 2: 1}[v]
    first, second, third, last = cut(main, [("e", g, 0), ("pv0", g, 3), ("sc", then, 0)])
    mask, v0 = ("mask", g), [("v0", g, t) for t in range(NT)]
    ri, pv, rb, no, cn0, gate0, cn1, gate1 = before
    elu, elu2 = finish(g)
    if v == 7:
        stats1, norm1, ht2, ht3, s2 = prepare(1)[1:6]
        side = [elu, stats1, elu2, norm1, stats, ht2, norm, ht3, s2, ht0, ht1, qk0, qk1, vp0, vp1]
    else:
        side = [elu, None, elu2, None, stats, None, norm, None, ht0, ht1, qk0, qk1, vp0, vp1]
    return merge(first, [ri, pv, mask, v0[0], v0[1], rb, v0[2], v0[3]], *SPREAD[f"{v}a"]) \
        + merge(second, [qk2, no, qk3, cn0, gate0, cn1, gate1], *SPREAD[f"{v}b"]) \
        + third[:1] + merge(third[1:], side, *SPREAD[f"{v}c"]) + last


AROUND = [s for v in (6, 7, 2) for s in visit(v)]
TURN = [s for v in (3, 4, 5) for s in visit(v)] + AROUND
PROLOGUE = [s for s in AROUND if s[1] < 4]

EVENTS = {
    "mask": ["mask_ready", "adj_used"], "maskt": ["maskt_made", "maskt_ready"],
    "stats": ["stats_ready", "rstd_ready"], "norm": ["normed"],
    "ht": ["ht_made", "ht_ready"],
    "s2": ["s2_made", "s2_ready"], "v0": ["v_made", "v_ready"], "vp": ["v_made", "v_ready"],
    "qk": ["qk_made", "hi_ready", "lo_ready"],
    "rows": ["rows_made", "rows_ready"], "cols": ["cols_made", "cols_ready"],
    "xp": ["xpa_ready", "xp_ready"], "xa": ["xhi_ready", "xrest_ready"],
    "xb": ["xmid_ready", "xlo_ready"], "ms": ["ms_made", "ms_ready"],
    "bc": ["bc_made", "edges_ready"], "pc": ["pc_made", "pc_ready", "head_ready"],
    "e": ["scores_moved", "probs_ready"],
    "sc": ["scores_made", "scores_moved", "probs_ready"],
    "tr": ["probst_made"],
    "pv": ["out_made"], "pv0": ["out0_made", "z_ready"],
    "ri": ["rinv_ready"], "rb": ["rb_made", "rb_ready"], "no": ["ot_ready"],
    "y": ["y_made", "x_ready"], "z2": ["z_ready"],
    "elu": ["elu_min", "elu_exp"], "elu2": ["elu_ready", "xsum_ready"],
    "cn": ["cn_made", "cn_used"], "gate": ["gate_made", "tanh_ready", "y_ready"],
}


def mover(step):
    return "act" if step[2] % 8 in (0, 2, 5, 6, 7) else "dve"


def events_of(step):
    own = EVENTS[step[0]]
    if step[0] == "tr":
        own = own + ["probst_by_" + mover(step)]
    return own


AT, PER = {}, {}
FIRST_AT, AHEAD = {}, {}
for steps, places, counts in ((PROLOGUE, FIRST_AT, AHEAD), (TURN, AT, PER)):
    for step in steps:
        for event in events_of(step):
            places[event, step] = counts.get(event, 0)
            counts[event] = counts.get(event, 0) + 1
LAST_DONE = {(event, step): len([1 for (e, s), n in AT.items() if e == event and n <= AT[event, step]
                                 and (e, s) not in FIRST_AT]) for event, step in AT}
START = {event: 2 * PER[event] - AHEAD.get(event, 0) for event in PER}

DELAY = {"act": {"sc": 4, "e": 4}}


def order(engine, steps):
    def key(n):
        kind = steps[n][0]
        return n + DELAY.get(engine, {}).get(kind, 0)
    return sorted(range(len(steps)), key=key)


MISC = ("ht", "s2", "v0", "pv0", "vp", "qk", "rows", "cols", "maskt", "ms", "rb", "y", "cn", "gate")
MISC_LAST = {"ht": "ht_ready", "s2": "s2_ready", "v0": "v_ready", "pv0": "z_ready",
             "vp": "v_ready", "qk": "lo_ready",
             "rows": "rows_ready", "cols": "cols_ready", "maskt": "maskt_ready", "ms": "ms_ready",
             "rb": "rb_ready", "y": "x_ready", "cn": "cn_used", "gate": "tanh_ready"}
assert len([s for s in TURN if s[0] in MISC]) % 2 == 0


def build(nc, x_in, adj_in, w0, w0t, a12_in, wq1, wk1, wv1, wo1, w2, w2t, a_gat, wq3, wk3, wv3, wg3, bg, out):
    with ExitStack() as ctx:
        def sb(name, shape, dt=F32):
            return ctx.enter_context(nc.sbuf_tensor(name, shape, dt))

        def ps(name, shape, dt=F32):
            return ctx.enter_context(nc.psum_tensor(name, shape, dt))

        def sem(name):
            return ctx.enter_context(nc.semaphore(name))

        x = [sb(f"x{g}", [P, NT, D]) for g in range(2)]
        mask = [sb(f"mask{g}", [P, NT, N], BF16) for g in range(2)]
        edge_t = [sb(f"edge_t{g}", [P, NT, N], BF16) for g in range(2)]
        hn = [sb(f"hn{g}", [P, NT, D]) for g in range(2)]
        ht = [sb(f"ht{g}", [P, DC, N]) for g in range(2)]
        val = [sb(f"val{g}", [P, NT, D + 1]) for g in range(2)]
        s2b = [sb(f"s2b{g}", [P, N]) for g in range(2)]
        rows = s2b
        fa = [sb(f"fa{g}", [P, NT, H]) for g in range(2)]
        fb = [sb(f"fb{g}", [P, NT, H]) for g in range(2)]
        ea = [sb(f"ea{g}", [P, NT, H]) for g in range(2)]
        eb = [sb(f"eb{g}", [P, NT, H]) for g in range(2)]
        sip = [sb(f"sip{g}", [P, NT, H]) for g in range(2)]
        nsj = [sb(f"nsj{g}", [P, NT, H]) for g in range(2)]
        adj = [sb(f"adj{i}", [P, N], I32) for i in range(2)]
        bn = sb("bn", [P, NT, 6])
        mv = sb("mv", [P, NT, 2])
        rstd = sb("rstd", [P, NT])
        vare = sb("vare", [P, NT])
        power = sb("power", [P, NT])
        split = sb("split", [P, 4, N], F32R)
        stack = [sb(f"stack{b}", [96, 2, 4, N], F32R) for b in range(2)]
        probs = [sb(f"probs{i}", [P, N]) for i in range(RING)]
        shift = sb("shift", [P, 4 * H])
        sums = [sb(f"sums{i}", [P, 2, 4, 4]) for i in range(2)]
        rinv = sb("rinv", [P, 4, 4])
        probs_t = [sb(f"probs_t{i}", [P, 4, NT, 2 * P]) for i in range(2)]
        edges = [probs_t[0][:, i, :, :].rearrange("p b c -> p (b c)").bitcast(BF16)
                 .rearrange("p (t n) -> p t n", t=NT) for i in range(4)]
        parts = probs_t[1][:, :, :, :].rearrange("p a b c -> p (a b c)").bitcast(BF16)
        part3 = [parts[:, k * NT * H * 2 * XW:(k + 1) * NT * H * 2 * XW]
                 .rearrange("p (t h c) -> p t h c", t=NT, h=H) for k in range(3)]
        rb = sb("rb", [P, N])
        ot = sb("ot", [P, DC, N])
        vx = sb("vx", [P, NT, H, 2 * XW])
        x0 = [vx[:, :, :, :].rearrange("p t h c -> p (t h c)")[:, NT * D * g:NT * D * (g + 1)]
              .rearrange("p (t d) -> p t d", t=NT) for g in range(2)]
        msum = sb("msum", [P, NT, H, XW])
        ht0 = msum[:, :, :, :].rearrange("p t h c -> p (t h c)")[:, 0:DC * N]\
            .rearrange("p (c n) -> p c n", c=DC)
        part = [sb(f"part{i}", [P, NT, 2 * XW]) for i in range(2)]
        diff = sb("diff", [P, NT, XW])
        numer = sb("numer", [P, NT, H, XW])
        numer_flat = numer[:, :, :, :].rearrange("p t h c -> p (t h c)")
        hn0 = numer_flat[:, 0:NT * D].rearrange("p (t d) -> p t d", t=NT)
        probs0_t = numer_flat[:, 0:2 * NT * P].rearrange("p (a c q) -> p a c q", a=2, c=NT)
        z = sb("z", [P, NT, D])
        ez = sb("ez", [P, NT, D])
        tanh = [ez[:, 2 * j:2 * j + 2, :] for j in range(2)]
        small = sb("small", [P, 4 * NT])
        w_s = {n: sb("w_" + n, [P, DC, D]) for n in ("q1", "k1", "v1", "o1", "2", "q3", "k3", "v3")}
        w0_s = sb("w0_s", [P, DC, D + 1])
        w0_2 = sb("w0_2", [P, DC, P])
        wg_s = sb("wg_s", [P, 4, D])
        wt_s = ez
        a12 = sb("a12", [P, DC, 2])
        adiag = sb("adiag", [P, DC, 40])
        wa = sb("wa", [P, DC, 40])
        bg_s = sb("bg_s", [1, D])
        ident = sb("ident", [P, P])
        ident_b = sb("ident_b", [P, P], BF16)
        ones = sb("ones", [1, P])

        pscore = [ps(f"pscore{i}", [P, N]) for i in range(3)]
        ptrans = [ps(f"ptrans{i}", [P, N]) for i in range(2)]
        pout = ps("pout", [P, N])
        pmisc = [ps(f"pmisc{i}", [P, N]) for i in range(2)]
        pmisc_b = [p[:, :].bitcast(BF16) for p in pmisc]

        S = {e: sem("s_" + e) for e in sorted({e for s in TURN for e in events_of(s)})}
        x_loaded = [sem(f"x_loaded{g}") for g in range(2)]
        adj_loaded = [sem(f"adj_loaded{i}") for i in range(2)]
        out_stored = [sem(f"out_stored{g}") for g in range(2)]
        stacked = [sem(f"stacked{b}") for b in range(2)]
        w_loaded = sem("w_loaded")
        credits = sem("credits")
        carried = sem("carried")
        setup_pool = sem("setup_pool")
        setup_pe = sem("setup_pe")
        setup_dve = sem("setup_dve")
        link_dve = sem("link_dve")
        link_act = sem("link_act")
        link_pool = sem("link_pool")

        class Walk:

            def __init__(self, eng, engine):
                self.eng, self.engine = eng, engine
                self.linked, self.base, self.per = 0, 0, 0
                self.i = -1
                self.first, self.last = True, False

            def at(self, event, step):
                if self.first:
                    here = (event, step) in FIRST_AT and TURN_AT[step] <= self.place
                    return START[event] + (FIRST_AT[event, step] + 1 if here else 0)
                last_turn = TURN_AT[step] > self.place
                if self.last and not last_turn:
                    return (self.i + 2) * PER[event] + LAST_DONE[event, step]
                return (self.i + 2) * PER[event] + AT[event, step] + 1 - (PER[event] if last_turn else 0)

            def next_link(self):
                self.linked += 1
                return (0 if self.first else self.i * self.per) + self.base + self.linked

            def run(self, eng_loop, do, per=0):
                for self.place in order(self.engine, TURN):
                    if TURN[self.place] in IN_PROLOGUE:
                        do(TURN[self.place])
                for event in AHEAD:
                    if event != "adj_used":
                        self.eng.wait_ge(S[event], 2 * PER[event])
                self.base, self.linked, self.per, self.first = self.linked, 0, per, False
                with eng_loop(0, PAIRS - 1) as self.i:
                    for self.place in order(self.engine, TURN):
                        do(TURN[self.place])
                assert self.linked == per, self.linked
                self.i, self.linked, self.last = PAIRS - 1, 0, True
                for self.place in order(self.engine, TURN):
                    if TURN[self.place] not in IN_PROLOGUE:
                        do(TURN[self.place])

        TURN_AT = {s: n for n, s in enumerate(TURN)}
        IN_PROLOGUE = set(PROLOGUE)

        def among(w, kinds):
            return [s for s in (PROLOGUE if w.first else TURN) if s[0] in kinds]

        def index(w, step, kinds):
            missing = len([s for s in TURN if s[0] in kinds]) - len(among(w, kinds))
            return among(w, kinds).index(step) + missing

        def back(w, step, kinds, k):
            steps = among(w, kinds)
            n = steps.index(step)
            return steps[n - k] if n >= k or not w.first else None

        def bank_user(w, step):
            steps = among(w, SCORES)
            n = steps.index(step)
            if n >= 3:
                return steps[n - 3]
            if w.first:
                return None
            return [s for m, s in enumerate(steps) if m % 3 == n % 3][-1]

        def misc_bank(w, step):
            return index(w, step, MISC) % 2

        SCORES = ("sc", "e")
        trs = [s for s in TURN if s[0] == "tr"]
        assert len(trs) % RING == 0
        moves = {s: "probst_by_" + mover(s) for s in trs}
        score_of = {s: ("sc" if layer(s[1]) in (1, 3) else "e",) + s[1:] for s in trs}

        def unpack(n):
            return n // 16, (n // 4) % 4, n % 4

        qks = [s for s in TURN if s[0] == "qk"]
        assert len(qks) % 2 == 0

        def masks(w, v):
            return 2 * w.i + 2 + graph(v)

        def adj_count(w, v, t):
            return (masks(w, v) + 2) * NT + t + 1

        def last_scores(w, step):
            _, v, b, _ = step
            here = TURN_AT[step]
            mine = [s for s in TURN if s[0] == "sc" and unpack(s[2])[0] == b]
            before = [s for s in mine if TURN_AT[s] < here]
            return before[-1] if before else mine[-1]

        def last_of(w, kind, step):
            mine = [s for s in TURN if s[0] == kind]
            before = [s for s in mine if TURN_AT[s] < TURN_AT[step]]
            return before[-1] if before else mine[-1]

        def stacks(w, step):
            _, v, b, _ = step
            same = [s for s in qks if s[2:] == (b, 1)]
            ahead = len([s for s in PROLOGUE if s[0] == "qk" and s[2:] == (b, 1)])
            turns = w.i if TURN_AT[step] <= w.place else w.i - 1
            return turns * (16 * 12 * len(same)) + 16 * 12 * (ahead + same.index(("qk", v, b, 1)) + 1) + 16

        def split_free(w, eng, step):
            last = back(w, step, ("qk",), 2)
            if last is not None:
                eng.wait_ge(stacked[last[2]], stacks(w, ("qk", last[1], last[2], 1)))

        def move_probs_t(w, step, copy):
            _, v, n = step
            bank = index(w, step, ("tr",)) % 2
            w.eng.wait_ge(S["probst_made"], w.at("probst_made", step))
            if layer(v) == 0:
                if n < 2:
                    w.eng.wait_ge(S["ht_made"], w.at("ht_made", ("ht", v, 1)))
                else:
                    w.eng.wait_ge(S["out0_made"], w.at("out0_made", ("pv0", v, n - 2)))
                return copy(probs0_t[:, n % 2, :, :], ptrans[bank][:, :].rearrange("p (c q) -> p c q", c=NT))
            b, t, head = unpack(n)
            buf = (n // 8) % 2
            if n % 8 < 2:
                if n // 8 >= 2:
                    w.eng.wait_ge(S["out_made"], w.at("out_made", ("pv", v, n // 8 - 2)))
                elif v % 2 == 1:
                    w.eng.wait_ge(S["out_made"], w.at("out_made", ("pv", v - 1, n // 8 + 2)))
                elif v == 2:
                    w.eng.wait_ge(S["out_made"], w.at("out_made", ("pv", 7, n // 8 + 2)))
                else:
                    w.eng.wait_ge(S["pc_made"], w.at("pc_made", ("pc", v - 1, H - 1)))
                    w.eng.wait_ge(S["out_made"], w.at("out_made", ("pv", 3, 3)))
            dst = probs_t[buf][:, head, :, (t % 2) * P:(t % 2 + 1) * P]
            return copy(dst, ptrans[bank][:, :].rearrange("p (c q) -> p c q", c=NT))

        block = ctx.enter_context(nc.Block())

        @block.sync
        def _(sp):
            for name, src in (("q1", wq1), ("k1", wk1), ("v1", wv1), ("o1", wo1), ("2", w2),
                              ("q3", wq3), ("k3", wk3), ("v3", wv3)):
                sp.dma_start(w_s[name][:, :, :], src.rearrange("(c p) n -> p c n", p=P)).then_inc(w_loaded, 16)
            sp.dma_start(w0_s[:, :, 0:D], w0.rearrange("(c p) n -> p c n", p=P)).then_inc(w_loaded, 16)
            sp.dma_start(wg_s[:, :, :], wg3.rearrange("(c p) n -> p c n", p=P)).then_inc(w_loaded, 16)
            sp.dma_start(wt_s[:, 0:2, :], w0t.rearrange("(c p) n -> p c n", p=P)).then_inc(w_loaded, 16)
            sp.dma_start(wt_s[:, 2:4, :], w2t.rearrange("(c p) n -> p c n", p=P)).then_inc(w_loaded, 16)
            sp.dma_start(a12[:, :, :], a12_in.rearrange("(c p) o -> p c o", p=P)).then_inc(w_loaded, 16)
            sp.dma_start(bg_s[:, :], bg.rearrange("(a n) -> a n", a=1)).then_inc(w_loaded, 16)
            sp.wait_ge(setup_pool, 1)
            for h in range(H):
                rows_h = slice(32 * (h % 4), 32 * (h % 4) + 32)
                sp.dma_start(adiag[rows_h, h // 4, h:h + 1],
                             a_gat[h, DK:2 * DK].rearrange("(p o) -> p o", o=1)).then_inc(w_loaded, 16)
                sp.dma_start(adiag[rows_h, h // 4, 32 + h:33 + h],
                             a_gat[h, 0:DK].rearrange("(p o) -> p o", o=1)).then_inc(w_loaded, 16)

            def load_x(pair, g):
                sp.dma_start(x0[g], x_in[pair, :, :].rearrange("(t p) d -> p t d", p=P))\
                    .then_inc(x_loaded[g], 16)

            def do(step):
                kind, v = step[0], step[1]
                g = graph(v)
                if kind == "mask":
                    index_in = 2 * w.i + 2 + g
                    for t in range(NT):
                        sp.wait_ge(S["adj_used"], adj_count(w, v, t - 2))
                        sp.dma_start(adj[t % 2][:, :], adj_in[index_in, t * P:(t + 1) * P, :])\
                            .then_inc(adj_loaded[t % 2], 16)
                if kind == "xb" and step[1:] == (5, NT - 1) and not w.last:
                    sp.wait_ge(S["xlo_ready"], w.at("xlo_ready", step))
                    for graph_in in range(2):
                        load_x(2 * w.i + 2 + graph_in, graph_in)
                if kind == "qk":
                    _, _, b, which = step
                    if which == 0:
                        return
                    sp.wait_ge(S["hi_ready"], w.at("hi_ready", step))
                    sp.sem_inc(carried, 1)
                    sp.wait_ge(S["lo_ready"], w.at("lo_ready", step))
                    sp.sem_inc(carried, 1)
                    last = last_scores(w, step)
                    sp.wait_ge(S["scores_made"], w.at("scores_made", last))
                    for r, (first, apart) in enumerate(((0, 2), (0, 3), (1, 1))):
                        for head in range(4):
                            rows_h = slice(32 * head, 32 * head + 32)
                            sp.dma_start(stack[b][32 * r:32 * r + 32, :, head, :].bitcast(F32),
                                         split[rows_h, first:first + apart + 1:apart, :].bitcast(F32))\
                                .then_inc(stacked[b], 16)
                if kind == "gate" and step[2] == 1:
                    sp.wait_ge(S["y_ready"], w.at("y_ready", step))
                    where = 2 * w.i + g
                    sp.dma_start(out[where, :, :].rearrange("(t p) d -> p t d", p=P), hn[g][:, :, :])\
                        .then_inc(out_stored[g], 16)

            load_x(0, 0)
            load_x(1, 1)
            sp.wait_ge(credits, 1)
            w = Walk(sp, "sp")
            w.run(sp.Fori, do)
            for g in range(2):
                sp.wait_ge(out_stored[g], 16 * (PAIRS + 1))
                sp.wait_ge(x_loaded[g], 16 * PAIRS)
                sp.wait_ge(adj_loaded[g], 16 * NT * PAIRS)
                b = g
                each = [s for s in TURN if s[0] == "qk" and s[2:] == (b, 1)]
                sp.wait_ge(stacked[b], 16 + 16 * 12 * PAIRS * len(each))

        @block.gpsimd
        def _(pool):
            gp = nc.gpsimd
            for e in S:
                pool.sem_inc(S[e], 2 * NT if e == "adj_used" else START[e])
            for s in stacked + out_stored:
                pool.sem_inc(s, 16)
            pool.sem_inc(credits, 1)
            gp.memset(adiag[:, :, :], 0.0).then_inc(setup_pool, 1)
            gp.memset(ident[:, :], 0.0)
            gp.memset(ident_b[:, :], 0.0)
            gp.memset(power[:, :], -0.5)
            gp.memset(ones[:, :], 1.0).then_inc(setup_pool, 1)
            pool.wait_ge(setup_pool, 2)
            gp.affine_select(out=ident[:, :], in_=ident[:, :], compare_op=ALU.not_equal, fill=1.0,
                             base=0, pattern=[[-1, P]], channel_multiplier=1).then_inc(setup_pool, 1)
            gp.affine_select(out=ident_b[:, :], in_=ident_b[:, :], compare_op=ALU.not_equal, fill=1.0,
                             base=0, pattern=[[-1, P]], channel_multiplier=1).then_inc(setup_pool, 1)

            w = Walk(pool, "pool")

            def do(step):
                kind, v = step[0], step[1]
                g = graph(v)
                if kind == "stats":
                    pool.wait_ge(S["stats_ready"], w.at("stats_ready", step))
                    pool.sem_inc(carried, 1)
                    gp.tensor_scalar(vare[:, :], mv[:, :, 1], EPS, None, op0=ALU.add).then_inc(link_pool, 1)
                    pool.wait_ge(link_pool, w.next_link())
                    gp.tensor_tensor(rstd[:, :], vare[:, :], power[:, :], ALU.pow)\
                        .then_inc(S["rstd_ready"], 1)
                if kind == "xp":
                    pool.wait_ge(S["v_ready"], w.at("v_ready", ("vp", v, 1)))
                    pool.wait_ge(S["cols_ready"], w.at("cols_ready", ("cols", v)))
                    pool.wait_ge(S["xlo_ready"], w.at("xlo_ready", ("xb", 9 - v, NT - 1)))
                    pool.wait_ge(S["xsum_ready"], w.at("xsum_ready", ("elu2", 1)))
                    for t in range(NT):
                        src = val[g][:, t, 0:D].rearrange("p (h d) -> p h d", h=H)
                        fac = fb[g][:, t, :].rearrange("p (h o) -> p h o", o=1).broadcast_to([P, H, DK])
                        gp.tensor_tensor(vx[:, t, :, XW:XW + DK], src, fac, ALU.mult)
                    for k, f in enumerate((fa, fb)):
                        ins = gp.tensor_copy(vx[:, :, :, k * XW + DK], f[g][:, :, :])
                    ins.then_inc(S["xp_ready"], 1)
                if kind == "elu2":
                    pool.wait_ge(S["elu_ready"], w.at("elu_ready", step))
                    gp.tensor_tensor(x[g][:, :, :], z[:, :, :], (x0[g] if layer(v) == 0 else x[g])[:, :, :], ALU.add)\
                        .then_inc(S["xsum_ready"], 1)
                if kind == "xb":
                    t = step[2]
                    pool.wait_ge(S["xmid_ready"], w.at("xmid_ready", step))
                    gp.tensor_tensor(part3[2][:, t, :, :], vx[:, t, :, :], part3[1][:, t, :, :], ALU.subtract)\
                        .then_inc(S["xlo_ready"], 1)
                if kind == "pc":
                    h = step[2]
                    pool.wait_ge(S["out0_made"], w.at("out0_made", ("pv0", 1, NT - 1)))
                    pool.wait_ge(S["pc_ready"], w.at("pc_ready", step))
                    pool.wait_ge(S["head_ready"], w.at("head_ready", last_of(w, "pc", step)))
                    pool.wait_ge(S["ms_ready"], w.at("ms_ready", ("ms", v, NT - 1)))
                    src = part[h % 2]
                    def col(t):
                        return t[g][:, :, h:h + 1].broadcast_to([P, NT, XW])
                    gp.tensor_tensor(diff[:, :, :], msum[:, :, h, :], src[:, :, XW:2 * XW], ALU.subtract).then_inc(link_pool, 1)
                    pool.wait_ge(link_pool, w.next_link())
                    gp.tensor_tensor(diff[:, :, :], diff[:, :, :], col(eb), ALU.mult).then_inc(link_pool, 1)
                    pool.wait_ge(link_pool, w.next_link())
                    gp.tensor_tensor(numer[:, :, h, :], src[:, :, 0:XW], col(ea), ALU.mult).then_inc(link_pool, 1)
                    pool.wait_ge(link_pool, w.next_link())
                    gp.tensor_tensor(numer[:, :, h, :], numer[:, :, h, :], diff[:, :, :], ALU.add)\
                        .then_inc(S["head_ready"], 1)

            w.run(pool.Fori, do, per=sum({"stats": 1, "pc": 3}.get(s[0], 0) for s in TURN))

        @block.scalar
        def _(act):
            sc = nc.scalar
            w = Walk(act, "act")
            act.wait_ge(credits, 1)

            def do(step):
                kind, v = step[0], step[1]
                g = graph(v)
                L = layer(v)
                bank = misc_bank(w, step) if kind in MISC else None
                if kind == "ht":
                    act.wait_ge(S["ht_made"], w.at("ht_made", step))
                    if L == 0:
                        act.wait_ge(S["head_ready"], w.at("head_ready", ("pc", 5, H - 1)))
                        act.wait_ge(S["v_made"], w.at("v_made", ("v0", 1 - v, NT - 1)))
                    dst = ht0 if L == 0 else ht[g]
                    sc.activation(dst[:, step[2], :], pmisc[bank][:, :], ACT.Relu).then_inc(S["ht_ready"], 1)
                if kind == "s2":
                    act.wait_ge(S["s2_made"], w.at("s2_made", step))
                    sc.activation(s2b[g][:, :], pmisc[bank][:, :], ACT.Copy).then_inc(S["s2_ready"], 1)
                if kind == "v0":
                    act.wait_ge(S["v_made"], w.at("v_made", step))
                    act.wait_ge(S["out_made"], w.at("out_made", ("pv", 6 + v, 3)))
                    sc.activation(val[g][:, step[2], :], pmisc[bank][:, 0:D + 1], ACT.Copy)\
                        .then_inc(S["v_ready"], 1)
                if kind == "vp":
                    j = step[2]
                    act.wait_ge(S["v_made"], w.at("v_made", step))
                    sc.activation(val[g][:, 2 * j:2 * j + 2, 0:D],
                                  pmisc[bank][:, :].rearrange("p (t d) -> p t d", t=2), ACT.Copy)\
                        .then_inc(S["v_ready"], 1)
                if kind == "qk":
                    act.wait_ge(S["qk_made"], w.at("qk_made", step))
                    split_free(w, act, step)
                    sc.activation(split[:, 2 * step[3], :], pmisc[bank][:, :], ACT.Copy).then_inc(S["hi_ready"], 1)
                if kind == "xa":
                    t = step[2]
                    act.wait_ge(S["xp_ready"], w.at("xp_ready", ("xp", v)))
                    act.wait_ge(S["xpa_ready"], w.at("xpa_ready", ("xp", v)))
                    event, last_step = ("out_made", ("pv", 3, 3)) if v == 4 else ("pc_made", ("pc", 4, H - 1))
                    act.wait_ge(S[event], w.at(event, last_step))
                    sc.activation(part3[0][:, t, :, :], vx[:, t, :, :], ACT.Copy).then_inc(S["xhi_ready"], 1)
                if kind == "xb":
                    t = step[2]
                    act.wait_ge(S["xrest_ready"], w.at("xrest_ready", ("xa", v, t)))
                    sc.activation(part3[1][:, t, :, :], vx[:, t, :, :], ACT.Copy).then_inc(S["xmid_ready"], 1)
                if kind == "ms":
                    t = step[2]
                    act.wait_ge(S["ms_made"], w.at("ms_made", step))
                    act.wait_ge(S["head_ready"], w.at("head_ready", ("pc", {4: 5, 5: 4}[v], H - 1)))
                    sc.activation(msum[:, t, :, :], pmisc[bank][:, 0:H * XW]
                                  .rearrange("p (h c) -> p h c", h=H), ACT.Copy).then_inc(S["ms_ready"], 1)
                if kind == "cols":
                    act.wait_ge(S["cols_made"], w.at("cols_made", step))
                    pc = pmisc[bank][:, 0:NT * 40].rearrange("p (t c) -> p t c", t=NT)
                    sc.activation(ea[g][:, :, :], pc[:, :, 32:40], ACT.Relu, scale=-1.0).then_inc(link_act, 1)
                    act.wait_ge(link_act, w.next_link())
                    sc.activation(eb[g][:, :, :], pc[:, :, 32:40], ACT.Relu).then_inc(link_act, 1)
                    act.wait_ge(link_act, w.next_link())
                    sc.activation(fa[g][:, :, :], pc[:, :, 0:8], ACT.Exp)
                    sc.activation(fb[g][:, :, :], pc[:, :, 0:8], ACT.Exp, scale=SLOPE2)
                    sc.activation(nsj[g][:, :, :], pc[:, :, 0:8], ACT.Copy, scale=-1.0)
                    sc.activation(sip[g][:, :, :], pc[:, :, 32:40], ACT.Copy)
                    sc.activation(ea[g][:, :, :], ea[g][:, :, :], ACT.Exp, scale=SLOPE2 - 1.0)
                    sc.activation(eb[g][:, :, :], eb[g][:, :, :], ACT.Exp, scale=SLOPE2 - 1.0)\
                        .then_inc(S["cols_ready"], 1)
                if kind == "pc":
                    h = step[2]
                    act.wait_ge(S["pc_made"], w.at("pc_made", step))
                    if h >= 2:
                        act.wait_ge(S["head_ready"], w.at("head_ready", ("pc", v, h - 2)))
                    sc.activation(part[h % 2][:, :, :], ptrans[h % 2][:, 0:NT * 2 * XW]
                                  .rearrange("p (t c) -> p t c", t=NT), ACT.Copy).then_inc(S["pc_ready"], 1)
                if kind == "e":
                    t = step[2]
                    n = index(w, step, SCORES)
                    act.wait_ge(S["scores_moved"], w.at("scores_moved", step))
                    act.wait_ge(S["z_ready"], w.at("z_ready", ("pv0", 1 - v, t)))
                    sc.activation(probs[n % RING][:, :], probs[n % RING][:, :], ACT.Exp,
                                  bias=small[:, 4 + t:5 + t], accum_out=small[:, 8 + t:9 + t])\
                        .then_inc(S["probs_ready"], 1)
                if kind == "sc":
                    n = index(w, step, SCORES)
                    b, t, head = unpack(step[2])
                    act.wait_ge(S["scores_moved"], w.at("scores_moved", step))
                    sc.activation(probs[n % RING][:, :], probs[n % RING][:, :], ACT.Exp, scale=-1.0,
                                  bias=shift[:, step[2]:step[2] + 1],
                                  accum_out=sums[g][:, b, t, head:head + 1]).then_inc(S["probs_ready"], 1)
                if kind == "tr" and mover(step) == "act":
                    move_probs_t(w, step, lambda o, i: sc.activation(o, i, ACT.Copy))\
                        .then_inc(S["probst_by_act"], 1)
                if kind == "rb":
                    act.wait_ge(S["rb_made"], w.at("rb_made", step))
                    sc.activation(rb[:, :], pmisc[bank][:, :], ACT.Copy).then_inc(S["rb_ready"], 1)
                if kind == "elu":
                    act.wait_ge(S["elu_min"], w.at("elu_min", step))
                    sc.activation(ez[:, :, :], ez[:, :, :], ACT.Exp).then_inc(S["elu_exp"], 1)
                if kind == "gate":
                    act.wait_ge(S["gate_made"], w.at("gate_made", step))
                    act.wait_ge(S["y_ready"], w.at("y_ready", ("gate", 13 - v, 1)))
                    act.wait_ge(S["elu_ready"], w.at("elu_ready", last_of(w, "elu2", step)))
                    sc.activation(tanh[step[2]], pmisc[bank][:, :].rearrange("p (t d) -> p t d", t=2),
                                  ACT.Tanh, scale=0.5).then_inc(S["tanh_ready"], 1)

            w.run(act.Fori, do, per=sum({"cols": 2}.get(s[0], 0) for s in TURN))

        LINKS = {"stats": 1, "e": 2, "rows": 2, "gate": 1, "z2": 2, "pv0": 1, "ri": 1}

        @block.vector
        def _(dve):
            vec = nc.vector
            w = Walk(dve, "dve")
            dve.wait_ge(credits, 1)
            dve.wait_ge(setup_pe, 1)
            vec.tensor_copy(w0_s[:, :, D], pmisc[0][:, 0:4].rearrange("p (c a) -> p c a", c=DC)[:, :, 0])\
                .then_inc(setup_dve, 1)
            for c in range(DC):
                vec.tensor_copy(w0_2[:, c, :], pmisc[0][:, 2 * c + 1:2 * c + 2].broadcast_to([P, P]))\
                    .then_inc(setup_dve, 1)
            vec.tensor_copy(wa[:, :, :], pmisc[0][:, 4:84].rearrange("p (c a) -> p c a", c=DC))\
                .then_inc(setup_dve, 1)

            def do(step):
                kind, v = step[0], step[1]
                g = graph(v)
                L = layer(v)
                bank = misc_bank(w, step) if kind in MISC else None
                if kind == "mask":
                    for t in range(NT):
                        dve.wait_ge(adj_loaded[t % 2], 16 * (2 * masks(w, v) + t // 2 + 1))
                        ins = vec.tensor_scalar(mask[g][:, t, :], adj[t % 2][:, :], 0.0, MASKED,
                                                op0=ALU.is_equal, op1=ALU.mult)
                        ins.then_inc(S["adj_used"], 1)
                    w.eng.wait_ge(S["adj_used"], adj_count(w, v, NT - 1))
                    vec.memset(small[:, 15:16], 0.0).then_inc(S["mask_ready"], 1)
                if kind == "maskt":
                    j = step[2]
                    dve.wait_ge(S["maskt_made"], w.at("maskt_made", step))
                    vec.tensor_scalar(edge_t[g][:, 2 * j:2 * j + 2, :],
                                      pmisc_b[bank].rearrange("p (t n) -> p t n", t=2),
                                      0.0, None, op0=ALU.is_equal).then_inc(S["maskt_ready"], 1)
                if kind == "stats":
                    if L == 0:
                        dve.wait_ge(x_loaded[g], (w.i + 2) * 16)
                    else:
                        event, last = ("x_ready", ("y", v - 2, 1)) if L == 2 else ("xsum_ready", ("elu2", v - 2))
                        dve.wait_ge(S[event], w.at(event, last))
                    dve.wait_ge(S["rstd_ready"], w.at("rstd_ready", last_of(w, "stats", step)))
                    dve.wait_ge(S["normed"], w.at("normed", last_of(w, "norm", step)))
                    source = x0[g] if L == 0 else x[g]
                    for t in range(NT):
                        ins = vec.bn_stats(bn[:, t, :], source[:, t, :])
                    ins.then_inc(link_dve, 1)
                    dve.wait_ge(link_dve, w.next_link())
                    dve.sem_inc(carried, 1)
                    for t in range(NT):
                        ins = vec.bn_aggr(mv[:, t, :], bn[:, t, :])
                    ins.then_inc(S["stats_ready"], 1)
                if kind == "norm":
                    dve.wait_ge(S["rstd_ready"], w.at("rstd_ready", ("stats", v)))
                    if L == 1:
                        dve.wait_ge(out_stored[g], 16 * (w.i + 2))
                    source, dst = (x0[g], hn0) if L == 0 else (x[g], hn[g])
                    if L == 0:
                        dve.wait_ge(S["out0_made"], w.at("out0_made", ("pv0", 1 - v, NT - 1)))
                    for t in range(NT):
                        ins = vec.tensor_scalar(dst[:, t, :], source[:, t, :], mv[:, t, 0:1], rstd[:, t:t + 1],
                                                op0=ALU.subtract, op1=ALU.mult)
                    ins.then_inc(S["normed"], 1)
                if kind == "qk":
                    split_free(w, dve, step)
                    dve.wait_ge(S["hi_ready"], w.at("hi_ready", step))
                    vec.tensor_tensor(split[:, 2 * step[3] + 1, :], pmisc[bank][:, :],
                                      split[:, 2 * step[3], :].bitcast(F32), ALU.subtract)\
                        .then_inc(S["lo_ready"], 1)
                if kind == "rows":
                    dve.wait_ge(S["rows_made"], w.at("rows_made", step))
                    pr = pmisc[bank]
                    vec.tensor_reduce(small[0:8, 12:13], pr[0:8, :], axis=AX_X, op=ALU.max)
                    vec.tensor_reduce(small[32:40, 12:13], pr[0:8, :], axis=AX_X, op=ALU.max).then_inc(link_dve, 1)
                    dve.wait_ge(link_dve, w.next_link())
                    vec.tensor_scalar(rows[g][0:8, :], pr[0:8, :], small[0:8, 12:13], None,
                                              op0=ALU.subtract).then_inc(link_dve, 1)
                    dve.wait_ge(link_dve, w.next_link())
                    vec.tensor_scalar(rows[g][32:40, :], pr[32:40, :], small[32:40, 12:13], None,
                                      op0=ALU.add).then_inc(S["rows_ready"], 1)
                if kind == "e":
                    t = step[2]
                    buf = probs[index(w, step, SCORES) % RING]
                    last = back(w, step, SCORES, RING)
                    dve.wait_ge(S["s2_ready"], w.at("s2_ready", ("s2", v)))
                    dve.wait_ge(S["v_ready"], w.at("v_ready", ("v0", v, NT - 1)))
                    dve.wait_ge(S["mask_ready"], w.at("mask_ready", ("mask", v)))
                    if last is not None:
                        dve.wait_ge(S["probs_ready"], w.at("probs_ready", last))
                    dve.sem_inc(carried, 1)
                    vec.tensor_tensor_reduce(out=buf[:, :], in0=s2b[g][:, :], in1=mask[g][:, t, :], scale=1.0,
                                             scalar=-BIG, op0=ALU.add, op1=ALU.max,
                                             accum_out=small[:, t:t + 1]).then_inc(link_dve, 1)
                    dve.wait_ge(link_dve, w.next_link())
                    s1 = val[g][:, t, D:D + 1]
                    vec.scalar_tensor_tensor(out=small[:, t:t + 1], in0=small[:, t:t + 1], scalar=-1.0,
                                             in1=s1, op0=ALU.mult, op1=ALU.subtract)
                    vec.tensor_scalar(buf[:, :], buf[:, :], s1, None, op0=ALU.add).then_inc(link_dve, 1)
                    dve.wait_ge(link_dve, w.next_link())
                    vec.scalar_tensor_tensor(out=small[:, 4 + t:5 + t], in0=small[:, t:t + 1], scalar=SLOPE0,
                                             in1=small[:, t:t + 1], op0=ALU.mult, op1=ALU.min)
                    vec.scalar_tensor_tensor(out=buf[:, :], in0=buf[:, :], scalar=SLOPE0, in1=buf[:, :],
                                             op0=ALU.mult, op1=ALU.max).then_inc(S["scores_moved"], 1)
                if kind == "sc":
                    n = index(w, step, SCORES)
                    b, t, head = unpack(step[2])
                    if step[2] == 0:
                        dve.wait_ge(S["mask_ready"], w.at("mask_ready", ("mask", g)))
                    last = back(w, step, SCORES, RING)
                    if last is not None:
                        last = ("tr",) + last[1:]
                        dve.wait_ge(S["probst_made"], w.at("probst_made", last))
                    dve.wait_ge(S["scores_made"], w.at("scores_made", step))
                    dve.sem_inc(carried, 1)
                    vec.tensor_tensor_reduce(out=probs[n % RING][:, :], in0=pscore[n % 3][:, :],
                                             in1=mask[g][:, t, :], scale=-SCALE, scalar=BIG,
                                             op0=ALU.add, op1=ALU.min,
                                             accum_out=shift[:, step[2]:step[2] + 1])\
                        .then_inc(S["scores_moved"], 1)
                if kind == "tr" and mover(step) == "dve":
                    move_probs_t(w, step, vec.tensor_copy).then_inc(S["probst_by_dve"], 1)
                if kind == "ri":
                    b = step[2]
                    dve.wait_ge(S["probs_ready"], w.at("probs_ready", ("sc", v, 16 * b + 15)))
                    vec.reciprocal(rinv[:, :, :], sums[g][:, b, :, :]).then_inc(link_dve, 1)
                    dve.wait_ge(link_dve, w.next_link())
                    rep = rinv[:, :, :].rearrange("p t (h o) -> p (t h) o", o=1).broadcast_to([P, 16, DK])
                    vec.tensor_copy(rb[:, :].rearrange("p (a d) -> p a d", d=DK), rep)\
                        .then_inc(S["rinv_ready"], 1)
                if kind == "no":
                    b = step[2]
                    dve.wait_ge(S["out_made"], w.at("out_made", ("pv", v, 2 * b + 1)))
                    dve.wait_ge(S["rb_ready"], w.at("rb_ready", ("rb", v, b)))
                    last = v - 1 if v % 2 == 1 else {2: 7, 6: 3}[v]
                    event, last_step = ("gate_made", ("gate", last, 1)) if layer(last) == 3 else ("y_made", ("y", last, 1))
                    dve.wait_ge(S[event], w.at(event, last_step))
                    if L == 1:
                        ins = vec.scalar_tensor_tensor(out=ot[:, b, :], in0=pout[:, :], scalar=0.0,
                                                       in1=rb[:, :], op0=ALU.max, op1=ALU.mult)
                    else:
                        ins = vec.tensor_tensor(ot[:, b, :], pout[:, :], rb[:, :], ALU.mult)
                    ins.then_inc(S["ot_ready"], 1)
                if kind == "y":
                    j = step[2]
                    dve.wait_ge(S["y_made"], w.at("y_made", step))
                    half = x[g][:, 2 * j:2 * j + 2, :]
                    vec.tensor_tensor(half, pmisc[bank][:, :].rearrange("p (t d) -> p t d", t=2), half, ALU.add)\
                        .then_inc(S["x_ready"], 1)
                if kind == "pv0":
                    t = step[2]
                    dve.wait_ge(S["out0_made"], w.at("out0_made", step))
                    dve.wait_ge(S["probs_ready"], w.at("probs_ready", ("e", v, t)))
                    dve.wait_ge(S["xsum_ready"], w.at("xsum_ready", ("elu2", 5 if v == 0 else 0)))
                    vec.reciprocal(small[:, t:t + 1], small[:, 8 + t:9 + t]).then_inc(link_dve, 1)
                    dve.wait_ge(link_dve, w.next_link())
                    vec.tensor_scalar(z[:, t, :], pmisc[bank][:, 0:D], small[:, t:t + 1], None, op0=ALU.mult)\
                        .then_inc(S["z_ready"], 1)
                if kind == "xp":
                    dve.wait_ge(S["v_ready"], w.at("v_ready", ("vp", v, 1)))
                    dve.wait_ge(S["cols_ready"], w.at("cols_ready", ("cols", v)))
                    dve.wait_ge(S["xlo_ready"], w.at("xlo_ready", ("xb", 9 - v, NT - 1)))
                    for t in range(NT):
                        src = val[g][:, t, 0:D].rearrange("p (h d) -> p h d", h=H)
                        fac = fa[g][:, t, :].rearrange("p (h o) -> p h o", o=1).broadcast_to([P, H, DK])
                        ins = vec.tensor_tensor(vx[:, t, :, 0:DK], src, fac, ALU.mult)
                    ins.then_inc(S["xpa_ready"], 1)
                if kind == "xa":
                    t = step[2]
                    dve.wait_ge(S["xhi_ready"], w.at("xhi_ready", step))
                    vec.tensor_tensor(vx[:, t, :, :], vx[:, t, :, :], part3[0][:, t, :, :], ALU.subtract)\
                        .then_inc(S["xrest_ready"], 1)
                if kind == "bc":
                    h = step[2]
                    dst = edges[h % 4]
                    dve.wait_ge(S["bc_made"], w.at("bc_made", step))
                    if h == 0:
                        dve.wait_ge(S["maskt_ready"], w.at("maskt_ready", ("maskt", v, 1)))
                    if h >= 4:
                        dve.wait_ge(S["pc_made"], w.at("pc_made", ("pc", v, h - 4)))
                    elif v == 5:
                        dve.wait_ge(S["pc_made"], w.at("pc_made", ("pc", 4, h + 4)))
                    else:
                        dve.wait_ge(S["out_made"], w.at("out_made", ("pv", 3, 2)))
                    for t in range(NT):
                        ins = vec.scalar_tensor_tensor(out=dst[:, t, :], in0=pscore[h % 3][:, :],
                                                       scalar=nsj[g][:, t, h:h + 1], in1=edge_t[g][:, t, :],
                                                       op0=ALU.is_gt, op1=ALU.mult)
                    ins.then_inc(S["edges_ready"], 1)
                if kind == "z2":
                    dve.wait_ge(S["head_ready"], w.at("head_ready", ("pc", v, H - 1)))
                    den = ez[:, 0, 0:NT * H].rearrange("p (t h) -> p t h", t=NT)
                    dve.wait_ge(S["elu_exp"], w.at("elu_exp", last_of(w, "elu", ("elu", v))))
                    dve.wait_ge(S["xsum_ready"], w.at("xsum_ready", ("elu2", v - 1) if v == 5 else ("elu2", 1)))
                    vec.tensor_scalar(den, numer[:, :, :, DK], 1e-37, None, op0=ALU.max).then_inc(link_dve, 1)
                    dve.wait_ge(link_dve, w.next_link())
                    vec.reciprocal(den, den).then_inc(link_dve, 1)
                    dve.wait_ge(link_dve, w.next_link())
                    for t in range(NT):
                        fac = den[:, t, :].rearrange("p (h o) -> p h o", o=1).broadcast_to([P, H, DK])
                        ins = vec.tensor_tensor(z[:, t, :].rearrange("p (h d) -> p h d", h=H),
                                                numer[:, t, :, 0:DK], fac, ALU.mult)
                    ins.then_inc(S["z_ready"], 1)
                if kind == "elu":
                    dve.wait_ge(S["z_ready"], w.at("z_ready", ("z2", v) if L == 2 else ("pv0", v, NT - 1)))
                    dve.wait_ge(S["tanh_ready"], w.at("tanh_ready", last_of(w, "gate", step)))
                    vec.tensor_scalar(ez[:, :, :], z[:, :, :], 0.0, None, op0=ALU.min).then_inc(S["elu_min"], 1)
                if kind == "elu2":
                    dve.wait_ge(S["elu_exp"], w.at("elu_exp", ("elu", v)))
                    vec.scalar_tensor_tensor(out=z[:, :, :], in0=ez[:, :, :], scalar=-1.0,
                                             in1=z[:, :, :], op0=ALU.add, op1=ALU.max)\
                        .then_inc(S["elu_ready"], 1)
                if kind == "cn":
                    j = step[2]
                    dve.wait_ge(S["cn_made"], w.at("cn_made", step))
                    c = pmisc[bank][:, :].rearrange("p (t d) -> p t d", t=2)
                    sl = slice(2 * j, 2 * j + 2)
                    vec.scalar_tensor_tensor(out=hn[g][:, sl, :], in0=hn[g][:, sl, :], scalar=0.0, in1=c,
                                             op0=ALU.max, op1=ALU.subtract)
                    vec.tensor_tensor(x[g][:, sl, :], c, x[g][:, sl, :], ALU.add).then_inc(S["cn_used"], 1)
                if kind == "gate":
                    j = step[2]
                    dve.wait_ge(S["tanh_ready"], w.at("tanh_ready", step))
                    dve.wait_ge(S["cn_used"], w.at("cn_used", ("cn", v, j)))
                    sl = slice(2 * j, 2 * j + 2)
                    vec.scalar_tensor_tensor(out=hn[g][:, sl, :], in0=tanh[j], scalar=1.0,
                                                     in1=hn[g][:, sl, :], op0=ALU.add, op1=ALU.mult).then_inc(link_dve, 1)
                    dve.wait_ge(link_dve, w.next_link())
                    vec.scalar_tensor_tensor(out=hn[g][:, sl, :], in0=hn[g][:, sl, :], scalar=0.5,
                                             in1=x[g][:, sl, :], op0=ALU.mult, op1=ALU.add)\
                        .then_inc(S["y_ready"], 1)

            w.run(dve.Fori, do, per=sum(LINKS.get(s[0], 0) for s in TURN))

        @block.tensor
        def _(pe):
            mm = nc.tensor.matmul
            w = Walk(pe, "pe")
            pe.wait_ge(w_loaded, 16 * (14 + 2 * H))
            pe.wait_ge(credits, 1)
            for c in range(DC):
                for o in range(DC):
                    mm(pmisc[0][:, 2 * c:2 * c + 2], wt_s[:, o, P * c:P * c + P], a12[:, o, :],
                       start=o == 0, stop=o == DC - 1)
            for c in range(DC):
                for o in range(DC):
                    last = mm(pmisc[0][:, 4 + 40 * c:44 + 40 * c], wt_s[:, 2 + o, P * c:P * c + P],
                              adiag[:, o, :], start=o == 0, stop=o == DC - 1)
            last.then_inc(setup_pe, 1)
            pe.wait_ge(setup_dve, 4)
            pe.wait_ge(setup_pool, 4)

            def do(step):
                kind, v = step[0], step[1]
                g = graph(v)
                L = layer(v)
                bank = misc_bank(w, step) if kind in MISC else None
                if kind in MISC:
                    last = back(w, step, MISC, 2)
                    if last is not None:
                        event = MISC_LAST[last[0]]
                        pe.wait_ge(S[event], w.at(event, last))
                hts = ht0 if L == 0 else ht[g]
                if kind == "ht":
                    j = step[2]
                    pe.wait_ge(S["normed"], w.at("normed", ("norm", v)))
                    normal = hn0 if L == 0 else hn[g]
                    for t in range(NT):
                        last = nc.tensor.transpose(pmisc[bank][:, P * t:P * t + P],
                                                   normal[:, t, P * j:P * j + P], ident[:, :])
                    last.then_inc(S["ht_made"], 1)
                if kind in ("s2", "v0", "vp", "rows", "qk"):
                    pe.wait_ge(S["ht_ready"], w.at("ht_ready", ("ht", v, 1)))
                if kind == "s2":
                    for c in range(DC):
                        last = mm(pmisc[bank][:, :], w0_2[:, c, :], hts[:, c, :], start=c == 0, stop=c == DC - 1)
                    last.then_inc(S["s2_made"], 1)
                if kind == "v0":
                    t = step[2]
                    for c in range(DC):
                        last = mm(pmisc[bank][:, 0:D + 1], hts[:, c, P * t:P * t + P], w0_s[:, c, :],
                                  start=c == 0, stop=c == DC - 1)
                    last.then_inc(S["v_made"], 1)
                if kind == "vp":
                    wv = w_s[{1: "v1", 2: "2", 3: "v3"}[L]]
                    for k in range(2):
                        t = 2 * step[2] + k
                        for c in range(DC):
                            last = mm(pmisc[bank][:, D * k:D * k + D], hts[:, c, P * t:P * t + P], wv[:, c, :],
                                      start=c == 0, stop=c == DC - 1)
                    last.then_inc(S["v_made"], 1)
                if kind == "qk":
                    _, _, b, which = step
                    wp = w_s["qk"[which] + str(L)]
                    for c in range(DC):
                        last = mm(pmisc[bank][:, :], wp[:, c, P * b:P * b + P], hts[:, c, :],
                                  start=c == 0, stop=c == DC - 1)
                    last.then_inc(S["qk_made"], 1)
                if kind == "rows":
                    for c in range(DC):
                        last = mm(pmisc[bank][0:40, :], wa[:, c, :], hts[:, c, :], start=c == 0, stop=c == DC - 1)
                    last.then_inc(S["rows_made"], 1)
                if kind == "cols":
                    pe.wait_ge(S["rows_ready"], w.at("rows_ready", ("rows", v)))
                    pe.sem_inc(carried, 1)
                    for t in range(NT):
                        last = nc.tensor.transpose(pmisc[bank][:, 40 * t:40 * t + 40],
                                                   rows[g][0:40, P * t:P * t + P], ident[0:40, 0:40])
                    last.then_inc(S["cols_made"], 1)
                if kind == "maskt":
                    j = step[2]
                    pe.wait_ge(S["mask_ready"], w.at("mask_ready", ("mask", g)))
                    for k in range(2):
                        for t in range(NT):
                            key = 2 * j + k
                            last = nc.tensor.transpose(pmisc_b[bank][:, N * k + P * t:N * k + P * t + P],
                                                       mask[g][:, t, P * key:P * key + P], ident_b[:, :])
                    last.then_inc(S["maskt_made"], 1)
                if kind == "sc":
                    n = index(w, step, SCORES)
                    b, t, head = unpack(step[2])
                    if step[2] % 16 == 0:
                        pe.wait_ge(stacked[b], stacks(w, ("qk", v, b, 1)))
                    last = bank_user(w, step)
                    if last is not None:
                        pe.wait_ge(S["scores_moved"], w.at("scores_moved", last))
                    if v == 6 and step[2] == 0:
                        pe.wait_ge(S["edges_ready"], w.at("edges_ready", ("bc", 5, H - 1)))
                    mm(pscore[n % 3][:, :], stack[b][:, 0, head, P * t:P * t + P], stack[b][:, 1, head, :],
                       start=True, stop=True).then_inc(S["scores_made"], 1)
                if kind == "tr":
                    at = index(w, step, ("tr",))
                    buf = index(w, score_of[step], SCORES)
                    pe.wait_ge(S["probs_ready"], w.at("probs_ready", score_of[step]))
                    last = back(w, step, ("tr",), 2)
                    if last is not None:
                        pe.wait_ge(S[moves[last]], w.at(moves[last], last))
                    if v == 6 and step[2] < 2:
                        pe.wait_ge(S["pc_ready"], w.at("pc_ready", ("pc", 5, H - 2 + step[2])))
                    for c in range(NT):
                        last = nc.tensor.transpose(ptrans[at % 2][:, P * c:P * c + P],
                                                   probs[buf % RING][:, P * c:P * c + P], ident[:, :])
                    last.then_inc(S["probst_made"], 1)
                if kind == "pv0":
                    t = step[2]
                    pe.wait_ge(S[moves["tr", v, t]], w.at(moves["tr", v, t], ("tr", v, t)))
                    pe.wait_ge(S["v_ready"], w.at("v_ready", ("v0", v, NT - 1)))
                    for c in range(NT):
                        last = mm(pmisc[bank][:, 0:D], probs0_t[:, t % 2, c, :], val[g][:, c, 0:D],
                                  start=c == 0, stop=c == NT - 1)
                    last.then_inc(S["out0_made"], 1)
                if kind == "pv":
                    quarter = step[2]
                    b, half = quarter // 2, quarter % 2
                    mine = [s for s in trs if s[1] == v and s[2] // 8 == quarter]
                    for last in {moves[s]: s for s in mine}.values():
                        pe.wait_ge(S[moves[last]], w.at(moves[last], last))
                    pe.wait_ge(S["v_ready"], w.at("v_ready", ("vp", v, 1)))
                    if half == 0:
                        last = ("no", v, 0) if b == 1 else ("no", {2: 7, 3: 2, 6: 3, 7: 6}[v], 1)
                        pe.wait_ge(S["ot_ready"], w.at("ot_ready", last))
                    for c in range(NT):
                        for head in range(4):
                            col = DK * (4 * b + head)
                            last = mm(pout[32 * head:32 * head + 32, 2 * P * half:2 * P * (half + 1)],
                                      val[g][:, c, col:col + DK], probs_t[quarter % 2][:, head, c, :],
                                      start=c == 0, stop=c == NT - 1, skip_group_check=True)
                    last.then_inc(S["out_made"], 1)
                if kind == "rb":
                    pe.wait_ge(S["rinv_ready"], w.at("rinv_ready", ("ri", *step[1:])))
                    for t in range(NT):
                        last = nc.tensor.transpose(pmisc[bank][:, P * t:P * t + P], rb[:, P * t:P * t + P],
                                                   ident[:, :])
                    last.then_inc(S["rb_made"], 1)
                if kind == "y":
                    pe.wait_ge(S["ot_ready"], w.at("ot_ready", ("no", v, 1)))
                    for k in range(2):
                        t = 2 * step[2] + k
                        for c in range(DC):
                            last = mm(pmisc[bank][:, D * k:D * k + D], ot[:, c, P * t:P * t + P],
                                      w_s["o1"][:, c, :], start=c == 0, stop=c == DC - 1)
                    last.then_inc(S["y_made"], 1)
                if kind == "cn":
                    pe.wait_ge(S["ot_ready"], w.at("ot_ready", ("no", v, 1)))
                    for k in range(2):
                        t = 2 * step[2] + k
                        for c in range(DC):
                            at = D * k + P * c
                            last = nc.tensor.transpose(pmisc[bank][:, at:at + P], ot[:, c, P * t:P * t + P],
                                                       ident[:, :])
                    last.then_inc(S["cn_made"], 1)
                if kind == "gate":
                    pe.wait_ge(S["ot_ready"], w.at("ot_ready", ("no", v, 1)))
                    for k in range(2):
                        t = 2 * step[2] + k
                        dst = pmisc[bank][:, D * k:D * k + D]
                        mm(dst, ones[0:1, :], bg_s[0:1, :], start=True, stop=False)
                        for c in range(4):
                            src = ot[:, c, P * t:P * t + P] if c < 2 else hts[:, c - 2, P * t:P * t + P]
                            last = mm(dst, src, wg_s[:, c, :], start=False, stop=c == 3)
                    last.then_inc(S["gate_made"], 1)
                if kind == "ms":
                    t = step[2]
                    pe.wait_ge(S["maskt_ready"], w.at("maskt_ready", ("maskt", v, 1)))
                    pe.wait_ge(S["xlo_ready"], w.at("xlo_ready", ("xb", v, NT - 1)))
                    for n in range(3 * NT):
                        c, k = divmod(n, 3)
                        last = mm(pmisc[bank][:, 0:H * XW], edge_t[g][:, c, P * t:P * t + P],
                                  part3[k][:, c, :, XW:2 * XW], start=n == 0, stop=n == 3 * NT - 1)
                    last.then_inc(S["ms_made"], 1)
                if kind == "bc":
                    h = step[2]
                    pe.wait_ge(S["cols_ready"], w.at("cols_ready", ("cols", v)))
                    if h >= 3:
                        pe.wait_ge(S["edges_ready"], w.at("edges_ready", ("bc", v, h - 3)))
                    elif v == 5:
                        pe.wait_ge(S["edges_ready"], w.at("edges_ready", ("bc", 4, H - 1)))
                    else:
                        pe.wait_ge(S["scores_moved"], w.at("scores_moved", ("sc", 3, 4 * H - 1)))
                    for t in range(NT):
                        last = nc.tensor.transpose(pscore[h % 3][:, P * t:P * t + P],
                                                   sip[g][:, t, h:h + 1].broadcast_to([P, P]), ident[:, :])
                    last.then_inc(S["bc_made"], 1)
                if kind == "pc":
                    h = step[2]
                    pe.wait_ge(S["edges_ready"], w.at("edges_ready", ("bc", v, h)))
                    if h >= 2:
                        pe.wait_ge(S["pc_ready"], w.at("pc_ready", ("pc", v, h - 2)))
                    elif v == 5:
                        pe.wait_ge(S["pc_ready"], w.at("pc_ready", ("pc", 4, 6 + h)))
                    else:
                        pe.wait_ge(S[moves["tr", 3, 30 + h]], w.at(moves["tr", 3, 30 + h], ("tr", 3, 30 + h)))
                    pe.wait_ge(S["xlo_ready"], w.at("xlo_ready", ("xb", v, NT - 1)))
                    for t in range(NT):
                        for n in range(3 * NT):
                            c, k = divmod(n, 3)
                            last = mm(ptrans[h % 2][:, 2 * XW * t:2 * XW * (t + 1)],
                                      edges[h % 4][:, c, P * t:P * t + P], part3[k][:, c, h, :],
                                      start=n == 0, stop=n == 3 * NT - 1)
                    last.then_inc(S["pc_made"], 1)

            w.run(pe.Fori, do)



def kernel(**inputs):
    import numpy as np
    import concourse.bacc as bacc
    from concourse.bass_utils import run_bass_kernel_spmd

    plain = lambda name: np.ascontiguousarray(inputs[name])
    turned = lambda name: np.ascontiguousarray(np.asarray(inputs[name]).T)
    arrays = {
        "x": plain("x"), "adj": plain("adj"), "w0": plain("L0_gnn_w"), "w0t": turned("L0_gnn_w"),
        "a12": np.concatenate([inputs["L0_gnn_a1"], inputs["L0_gnn_a2"]], axis=1),
        "wq1": plain("L1_gnn_Wq"), "wk1": plain("L1_gnn_Wk"), "wv1": plain("L1_gnn_Wv"), "wo1": plain("L1_gnn_Wo"),
        "w2": plain("L2_gnn_W"), "w2t": turned("L2_gnn_W"), "a_gat": plain("L2_gnn_a"),
        "wq3": turned("L3_gnn_Wq"), "wk3": turned("L3_gnn_Wk"), "wv3": turned("L3_gnn_Wv"),
        "wg3": turned("L3_gnn_Wg"), "bg": plain("L3_gnn_bg"),
    }
    nc = bacc.Bacc("TRN2", target_bir_lowering=False, num_devices=1)
    args = [nc.dram_tensor("in_" + n, a.shape, mybir.dt.from_np(a.dtype), kind="ExternalInput").ap()
            for n, a in arrays.items()]
    result = nc.dram_tensor("result", (B, N, D), F32, kind="ExternalOutput").ap()
    build(nc, *args, result)
    got = run_bass_kernel_spmd(nc, [{"in_" + n: a for n, a in arrays.items()}], core_ids=[0])
    return got.results[0]["result"]
```
